# Optimizing a Trainium2 kernel written in Bass

```python
import numpy as np
import jax
import jax.numpy as jnp

def _softmax(x, axis=-1):
    return jax.nn.softmax(x, axis=axis)

def _gelu(x):
    return jax.nn.gelu(x, approximate=True)

def _silu(x):
    return jax.nn.silu(x)

def _sigmoid(x):
    return jax.nn.sigmoid(x)

def _layernorm(x, axis=-1, eps=1e-05):
    m = jnp.mean(x, axis=axis, keepdims=True)
    v = jnp.var(x, axis=axis, keepdims=True)
    return (x - m) / jnp.sqrt(v + eps)

def _scatter_add(tgt, idx, src, axis=0):
    return tgt.at[idx].add(src)

def _segment_sum(src, seg, n):
    return jax.ops.segment_sum(src, seg, n)
kernel_name = 'mk_lm_tower_d1_tok_ids1024_r4_139ce8'

def setup_inputs(seed: int=0):
    np.random.seed(seed)
    _w = jnp.asarray

    def _rec_inputs():
        import jax
        import jax.numpy as jnp
        _rk = jax.random.key(seed)
        x = jax.random.randint(jax.random.fold_in(_rk, 1), (32, 128), 0, 127995, jnp.int32)
        return x
    x = _rec_inputs()

    def _L0_tok_setup():
        import jax, jax.numpy as jnp
        import numpy as np
        VOCAB_SIZE = 32000
        NUM_BUCKETS = 16384
        EMB_RANK = 64
        MODEL_DIM = 256
        key = jax.random.key(seed)
        k_tok, k_w, k_p = jax.random.split(key, 3)
        token_ids = jax.random.randint(k_tok, (8, 1024), 0, VOCAB_SIZE, dtype=jnp.int64)
        weight = 0.02 * jax.random.normal(k_w, (NUM_BUCKETS, EMB_RANK), dtype=jnp.float32)
        proj = 0.02 * jax.random.normal(k_p, (EMB_RANK, MODEL_DIM), dtype=jnp.float32)
        return {'token_ids': token_ids, 'weight': weight, 'proj': proj}
    _L0_tok_all = _L0_tok_setup()
    _L0_tok_in = {k: v for k, v in _L0_tok_all.items() if k in ('weight', 'proj')}
    del _L0_tok_all

    def _L0_attn_setup():
        import jax, jax.numpy as jnp
        import numpy as np
        import math
        D_MODEL = 256
        NUM_HEADS = 16
        HEAD = D_MODEL // NUM_HEADS
        EPS = 1e-05

        def _layernorm(x, w, b):
            mean = jnp.mean(x, axis=-1, keepdims=True)
            var = jnp.var(x, axis=-1, keepdims=True)
            return (x - mean) * w / jnp.sqrt(var + EPS) + b
        key = jax.random.key(seed)
        ks = jax.random.split(key, 5)
        x = jax.random.normal(ks[0], (2, 512, D_MODEL), dtype=jnp.float32)
        wq = jax.random.uniform(ks[1], (NUM_HEADS, D_MODEL, HEAD), dtype=jnp.float32) * 0.02
        wk = jax.random.uniform(ks[2], (NUM_HEADS, D_MODEL, HEAD), dtype=jnp.float32) * 0.02
        wv = jax.random.uniform(ks[3], (NUM_HEADS, D_MODEL, HEAD), dtype=jnp.float32) * 0.02
        wo = jax.random.uniform(ks[4], (D_MODEL, D_MODEL), dtype=jnp.float32) * 0.02
        ln_w = jnp.ones((D_MODEL,), dtype=jnp.float32)
        ln_b = jnp.zeros((D_MODEL,), dtype=jnp.float32)
        return {'x': x, 'ln_w': ln_w, 'ln_b': ln_b, 'wq': wq, 'wk': wk, 'wv': wv, 'wo': wo}
    _L0_attn_all = _L0_attn_setup()
    _L0_attn_in = {k: v for k, v in _L0_attn_all.items() if k in ('ln_w', 'ln_b', 'wq', 'wk', 'wv', 'wo')}
    del _L0_attn_all

    def _L0_ffn_setup():
        import jax, jax.numpy as jnp
        import numpy as np
        H = 256
        I = 704
        E = 8
        TOP_K = 2

        def _moe(hidden_states, router_w, gate_w, up_w, down_w):
            B, S, Hd = hidden_states.shape
            x = hidden_states.reshape(-1, Hd)
            logits = x @ router_w.T
            probs = jax.nn.softmax(logits.astype(jnp.float32), axis=-1)
            top_w, top_idx = jax.lax.top_k(probs, TOP_K)
            top_w = top_w.astype(x.dtype)
            onehot = jax.nn.one_hot(top_idx, E, dtype=x.dtype)
            w_te = jnp.einsum('tk,tke->te', top_w, onehot)
            g = jnp.einsum('th,eih->tei', x, gate_w)
            u = jnp.einsum('th,eih->tei', x, up_w)
            h = jax.nn.silu(g) * u
            y = jnp.einsum('tei,ehi,te->th', h, down_w, w_te)
            return y.reshape(B, S, Hd)
        key = jax.random.key(seed)
        ks = jax.random.split(key, 5)
        s = 0.02
        return {'hidden_states': jax.random.normal(ks[0], (2, 256, H), dtype=jnp.float32), 'router_w': jax.random.normal(ks[1], (E, H), dtype=jnp.float32) * s, 'gate_w': jax.random.normal(ks[2], (E, I, H), dtype=jnp.float32) * s, 'up_w': jax.random.normal(ks[3], (E, I, H), dtype=jnp.float32) * s, 'down_w': jax.random.normal(ks[4], (E, H, I), dtype=jnp.float32) * s}
    _L0_ffn_all = _L0_ffn_setup()
    _L0_ffn_in = {k: v for k, v in _L0_ffn_all.items() if k in ('router_w', 'gate_w', 'up_w', 'down_w')}
    del _L0_ffn_all
    return {'x': x, 'L0_tok_weight': _L0_tok_in['weight'], 'L0_tok_proj': _L0_tok_in['proj'], 'L0_attn_ln_w': _L0_attn_in['ln_w'], 'L0_attn_ln_b': _L0_attn_in['ln_b'], 'L0_attn_wq': _L0_attn_in['wq'], 'L0_attn_wk': _L0_attn_in['wk'], 'L0_attn_wv': _L0_attn_in['wv'], 'L0_attn_wo': _L0_attn_in['wo'], 'L0_ffn_router_w': _L0_ffn_in['router_w'], 'L0_ffn_gate_w': _L0_ffn_in['gate_w'], 'L0_ffn_up_w': _L0_ffn_in['up_w'], 'L0_ffn_down_w': _L0_ffn_in['down_w']}

def reference(x, L0_tok_weight, L0_tok_proj, L0_attn_ln_w, L0_attn_ln_b, L0_attn_wq, L0_attn_wk, L0_attn_wv, L0_attn_wo, L0_ffn_router_w, L0_ffn_gate_w, L0_ffn_up_w, L0_ffn_down_w):
    import jax
    import jax.numpy as jnp

    def _L0_tok_ref(token_ids, weight, proj):
        import jax, jax.numpy as jnp
        import numpy as np
        VOCAB_SIZE = 32000
        NUM_BUCKETS = 16384
        EMB_RANK = 64
        MODEL_DIM = 256
        h1 = (token_ids * 31 + 7) % NUM_BUCKETS
        h2 = (token_ids * 131 + 13) % NUM_BUCKETS
        e1 = weight[h1]
        e2 = weight[h2]
        out = 0.5 * (jnp.einsum('bsr,rd->bsd', e1, proj) + jnp.einsum('bsr,rd->bsd', e2, proj))
        return out

    def _L0_attn_ref(x, ln_w, ln_b, wq, wk, wv, wo):
        import jax, jax.numpy as jnp
        import numpy as np
        import math
        D_MODEL = 256
        NUM_HEADS = 16
        HEAD = D_MODEL // NUM_HEADS
        EPS = 1e-05

        def _layernorm(x, w, b):
            mean = jnp.mean(x, axis=-1, keepdims=True)
            var = jnp.var(x, axis=-1, keepdims=True)
            return (x - mean) * w / jnp.sqrt(var + EPS) + b
        y = _layernorm(x, ln_w, ln_b)
        seq_len = y.shape[-2]
        q = jnp.einsum('bsd,hde->bhse', y, wq)
        k = jnp.einsum('bsd,hde->bhse', y, wk)
        v = jnp.einsum('bsd,hde->bhse', y, wv)
        scores = jnp.einsum('bhse,bhte->bhst', q, k) / math.sqrt(HEAD)
        causal = jnp.triu(jnp.full((seq_len, seq_len), -jnp.inf, dtype=scores.dtype), k=1)
        scores = scores + causal
        weights = jax.nn.softmax(scores, axis=-1)
        attn = jnp.einsum('bhst,bhte->bshe', weights, v)
        attn = attn.reshape(*attn.shape[:-2], -1)
        out = attn @ wo
        return out + x

    def _L0_ffn_ref(hidden_states, router_w, gate_w, up_w, down_w):
        import jax, jax.numpy as jnp
        import numpy as np
        H = 256
        I = 704
        E = 8
        TOP_K = 2

        def _moe(hidden_states, router_w, gate_w, up_w, down_w):
            B, S, Hd = hidden_states.shape
            x = hidden_states.reshape(-1, Hd)
            logits = x @ router_w.T
            probs = jax.nn.softmax(logits.astype(jnp.float32), axis=-1)
            top_w, top_idx = jax.lax.top_k(probs, TOP_K)
            top_w = top_w.astype(x.dtype)
            onehot = jax.nn.one_hot(top_idx, E, dtype=x.dtype)
            w_te = jnp.einsum('tk,tke->te', top_w, onehot)
            g = jnp.einsum('th,eih->tei', x, gate_w)
            u = jnp.einsum('th,eih->tei', x, up_w)
            h = jax.nn.silu(g) * u
            y = jnp.einsum('tei,ehi,te->th', h, down_w, w_te)
            return y.reshape(B, S, Hd)
        return _moe(hidden_states, router_w, gate_w, up_w, down_w)
    h = _L0_tok_ref(x, L0_tok_weight, L0_tok_proj)
    h = h + _L0_attn_ref(_layernorm(h, axis=-1), L0_attn_ln_w, L0_attn_ln_b, L0_attn_wq, L0_attn_wk, L0_attn_wv, L0_attn_wo)
    h = h + _L0_ffn_ref(_layernorm(h, axis=-1), L0_ffn_router_w, L0_ffn_gate_w, L0_ffn_up_w, L0_ffn_down_w)
    return h

_drawn_inputs = setup_inputs


def setup_inputs(seed=0):
    import zlib

    import numpy as np

    out = dict(_drawn_inputs(seed))
    spreads = {'L0_attn_ln_w': (1.0, 0.2), 'L0_attn_ln_b': (0.0, 0.1)}
    factors = {'L0_attn_wq': 8.0,
     'L0_attn_wk': 8.0,
     'L0_attn_wv': 6.453,
     'L0_attn_wo': 8.0,
     'L0_ffn_router_w': 5.119,
     'L0_ffn_gate_w': 4.57,
     'L0_ffn_up_w': 4.459,
     'L0_ffn_down_w': 4.468}
    for name, (base, spread) in spreads.items():
        noise = np.random.default_rng([zlib.crc32(name.encode()), seed]).standard_normal(out[name].shape)
        drawn = base * np.exp(spread * noise) if base else spread * noise
        out[name] = jnp.asarray(drawn.astype(out[name].dtype))
    for name, factor in factors.items():
        out[name] = (out[name] * factor).astype(out[name].dtype)
    return out
```

```python
from contextlib import ExitStack

import concourse.bass as bass
from concourse import mybir

F32 = mybir.dt.float32
BF16 = mybir.dt.bfloat16
I32 = mybir.dt.int32
ALU = mybir.AluOpType
ACT = mybir.ActivationFunctionType
AX = mybir.AxisListType.X

P = 128
SEQS, SEQ = 32, 128
BUCKETS, RANK = 16384, 64
D, KC = 256, 2
HEADS, HD = 16, 16
EXPERTS, INNER = 8, 704
HALF = INNER // 2
CHUNKS = (128, 128, 96)
EPS = 1e-5
NEG = -1e30
QUARTERS, QH = 4, 4
VW = HD + 1
AVN = 96
RN = 96
PAIRS = 2 * SEQS
TILES = (2 * SEQS * SEQ + EXPERTS * (P - 1)) // P
TRASH = PAIRS * P
GROUP = 8
SCALE = HD ** -0.5


class At:

    def __init__(self, k, u):
        self.k, self.u = k, u
        self.i = 2 * k + u

    def plus(self, n):
        u = self.u + n
        return At(self.k + u // 2 if u // 2 else self.k, u % 2)


def wait(eng, sem, value):
    if isinstance(value, int) and value <= 0:
        return
    eng.wait_ge(sem, value)


def wait_apart(eng, sem, value, met):
    if not isinstance(value, int):
        value = eng.to_reg(value)
    eng.wait_ge(*met)
    eng.wait_ge(sem, value)


def build(nc, tokens, emb, proj, ln_w, ln_b, wq, wk, wv, wo, router, gate_up, down, out):
    xs = nc.dram_tensor("normed_tokens", (SEQS * SEQ, D), F32).ap()
    ys = nc.dram_tensor("expert_rows", (TRASH + TILES * P, D), F32).ap()

    ctx = ExitStack()
    with ctx:
        def sb(name, shape, dt=F32):
            return ctx.enter_context(nc.sbuf_tensor(name, shape, dt))

        def sem(name):
            return ctx.enter_context(nc.semaphore(name))

        bank = [ctx.enter_context(nc.psum_tensor(f"bank{n}", [P, 512], F32)) for n in range(8)]

        ident = sb("ident", [P, P])
        identb = sb("identb", [P, P], BF16)
        causal = sb("causal", [P, QH * P], BF16)
        headmask = sb("headmask", [P, 8])
        before = sb("before", [P, P], BF16)
        onesb = sb("onesb", [P, P], BF16)
        iota_lo = sb("iota_lo", [P, P])
        iota_tile = sb("iota_tile", [P, TILES])
        iota_trash = sb("iota_trash", [P, TILES])
        iota_pair = sb("iota_pair", [P, PAIRS])
        place1 = sb("place1", [P, 1])
        low_first = sb("low_first", [P, EXPERTS])
        ln_mul = sb("ln_mul", [P, 2])
        ln_add = sb("ln_add", [P, 2])
        minus_half = sb("minus_half", [P, 2])

        proj_s = sb("proj_s", [P, D])
        wqk_s = sb("wqk_s", [P, KC, 2 * D])
        wv_s = sb("wv_s", [P, KC, D])
        wo_s = sb("wo_s", [P, KC, D])
        lnw_s = sb("lnw_s", [P, KC])
        lnb_s = sb("lnb_s", [P, KC])
        rw_s = sb("rw_s", [P, KC, RN])
        gu_s = sb("gu_s", [P, EXPERTS, KC, 2, 2, HALF])
        tok_s = sb("tok_s", [P, SEQS], I32)
        hash_s = sb("hash_s", [P, SEQS, 2], I32)
        hidden = sb("hidden", [P, SEQS, D])
        logits = sb("logits", [P, SEQS, EXPERTS])

        region = sb("region", [P, EXPERTS * 6 * D])
        down_s = region[:, :].rearrange("p (e c n) -> p e c n", e=EXPERTS, c=6)
        used = [0]

        def part(*shape, dt=F32):
            n = 1
            for s in shape:
                n *= s
            words = n if dt != BF16 else n // 2
            a = region[:, used[0]:used[0] + words]
            used[0] += words
            assert used[0] <= EXPERTS * 6 * D
            if dt != F32:
                a = a.bitcast(dt)
            if len(shape) == 2:
                a = a.rearrange("p (a b) -> p a b", a=shape[0])
            if len(shape) == 3:
                a = a.rearrange("p (a b c) -> p a b c", a=shape[0], b=shape[1])
            return a

        pair_emb = part(2, 2 * RANK)
        emb_t = part(P)
        z = part(D)
        y_t = part(KC, P)
        q_masked = part(HEADS, P)
        k_t = part(2, KC, P)
        v_one = part(2, HEADS * VW + AVN)
        shifted = part(2, QH * P)
        probs = part(2, QH * P)
        probs_t = part(2, QH * P)
        attn = part(D)
        attn_t = part(KC, P)
        x2 = sb("x2", [P, 2, D])
        x2_t = part(KC, P)
        rowmax = part(2, QH)
        recip = part(HEADS)
        bnF, mvF, aF, rF, nmF = part(6), part(2), part(2), part(2), part(2)
        bnO, mvO, aO, rO, nmO = part(6), part(2), part(2), part(2), part(2)
        gathered_idx = sb("gathered_idx", [P, 2, 2], I32)

        used[0] = 0
        NE = SEQS * EXPERTS
        top1, top2, rmask_a, work_a = part(SEQS), part(SEQS), part(SEQS, EXPERTS), part(SEQS, EXPERTS)
        rmask_b, work_b, lg2 = part(SEQS, EXPERTS), part(SEQS, EXPERTS), part(SEQS, EXPERTS)
        both = part(SEQS + 1, EXPERTS)
        cum_a, cum_b = part(SEQS, EXPERTS), part(SEQS, EXPERTS)
        both_h = part(SEQS, EXPERTS, dt=BF16)
        cum_h = part(SEQS + 1, EXPERTS, dt=BF16)
        count_f, count_i = part(EXPERTS), part(EXPERTS, dt=I32)
        tiles_i, tiles_f = part(EXPERTS, dt=I32), part(EXPERTS)
        ends, ends2, base = part(EXPERTS), part(EXPERTS), part(EXPERTS)
        pos_f, pos_i = part(SEQS, 2), part(SEQS, 2, dt=I32)
        hi_i, lo_i = part(SEQS, 2, dt=I32), part(SEQS, 2, dt=I32)
        hi_f, lo_f = part(SEQS, 2), part(SEQS, 2)
        onehot_lo = part(2, GROUP * P, dt=BF16)
        onehot_hi = part(2, GROUP * 72)
        onehot_hv = part(2, 2 * GROUP * 72, dt=BF16)
        tab = part(2, TILES)
        pair_i, half_i = part(TILES, dt=I32), part(TILES, dt=I32)
        half_f, place_f, empty = part(TILES), part(TILES), part(TILES)
        cmp_f = part(TILES, EXPERTS)
        exp_f = part(TILES)
        top_w = sb("top_w", [P, 2, SEQS])
        esum = sb("esum", [P, SEQS])
        tok_of = sb("tok_of", [P, TILES], I32)
        row_of = sb("row_of", [P, TILES], I32)
        exp_of = sb("exp_of", [1, TILES], I32)

        tok_idx = sb("tok_idx", [P, 2], I32)
        row_idx = sb("row_idx", [P, 2], I32)
        xe = sb("xe", [P, 2, D])
        xe_t = sb("xe_t", [P, 2, KC, P])
        silu = sb("silu", [P, 2, HALF])
        h_s = sb("h_s", [P, 2, HALF])
        h_t = sb("h_t", [P, 2, 3, P])
        y_s = sb("y_s", [P, 2, D])

        ld_tok, ld_att, ld_gu, ld_down = sem("ld_tok"), sem("ld_att"), sem("ld_gu"), sem("ld_down")
        const_v, const_p, const_q = sem("const_v"), sem("const_p"), sem("const_q")
        hashed = sem("hashed")
        idx_ready = sem("idx_ready")
        emb_in = [sem("emb_in0"), sem("emb_in1")]
        embT_ps, embT_sb, h_ps = sem("embT_ps"), sem("embT_sb"), sem("h_ps")
        f_bn, f_mv, f_a, f_pow, f_nm, f_r1, z_sb, base_sb = (
            sem(n) for n in ("f_bn", "f_mv", "f_a", "f_pow", "f_nm", "f_r1", "z_sb", "base_sb"))
        zT_ps, yT_sb, qk_ps, k_sb, q_sb, v_ps, v_sb = (
            sem(n) for n in ("zT_ps", "yT_sb", "qk_ps", "k_sb", "q_sb", "v_ps", "v_sb"))
        s_ps, max_sb, shift_sb, exp_sb, pT_ps, pT_sb, av_ps = (
            sem(n) for n in ("s_ps", "max_sb", "shift_sb", "exp_sb", "pT_ps", "pT_sb", "av_ps"))
        rec_sb, attn_sb, attnT_ps, attnT_sb, o_ps, hid_sb = (
            sem(n) for n in ("rec_sb", "attn_sb", "attnT_ps", "attnT_sb", "o_ps", "hid_sb"))
        o_bn, o_mv, o_a, o_pow, o_nm, x2_sb = (
            sem(n) for n in ("o_bn", "o_mv", "o_a", "o_pow", "o_nm", "x2_sb"))
        x2_out = [sem("x2_out0"), sem("x2_out1")]
        x2T_ps, x2T_sb, lg_ps, lg_sb = sem("x2T_ps"), sem("x2T_sb"), sem("lg_ps"), sem("lg_sb")
        route, rank_ps, wexp, wexp_in = sem("route"), sem("rank_ps"), sem("wexp"), sem("wexp_in")
        oh_lo, oh_hi, oh_hp, oh_hc, tab_mm = (
            sem(n) for n in ("oh_lo", "oh_hi", "oh_hp", "oh_hc", "tab_mm"))
        routed, counted = sem("routed"), sem("counted")
        tidx, ridx = sem("tidx"), sem("ridx")
        xe_in = [sem("xe_in0"), sem("xe_in1")]
        xeT_ps, xeT_sb = sem("xeT_ps"), sem("xeT_sb")
        gu_ps, silu_sb, hid2_sb, hT_ps, hT_sb, y_ps, y_sb = (
            sem(n) for n in ("gu_ps", "silu_sb", "hid2_sb", "hT_ps", "hT_sb", "y_ps", "y_sb"))
        y_out = [sem("y_out0"), sem("y_out1")]
        comb_in = [sem("comb_in0"), sem("comb_in1")]
        comb_a, comb_b = sem("comb_a"), sem("comb_b")
        fin = [sem("fin0"), sem("fin1")]

        block = ctx.enter_context(nc.Block())

        S = [bank[0], bank[1]]
        PT = [bank[2], bank[3]]
        AV, FB, VB, OB = bank[4], bank[5], bank[6], bank[7]
        N_ATT = 16 * 9
        N_EXP_CONST = 12

        def run_sequences(eng, step):
            step(At(0, 0), None, None)
            step(At(0, 1), At(0, 0), None)
            step(At(1, 0), At(0, 1), At(0, 0))
            with eng.Fori(1, SEQS // 2 - 1) as k:
                step(At(k, 0).plus(1), At(k, 0), At(k, 0).plus(-1))
                step(At(k, 1).plus(1), At(k, 1), At(k, 0))
            last = SEQS - 1
            step(At(last // 2, 1), At(last // 2, 0), At(last // 2 - 1, 1))
            step(None, At(last // 2, 1), At(last // 2, 0))
            step(None, None, At(last // 2, 1))

        @block.sync
        def _(eng):
            eng.dma_start(tok_s[:, :], tokens).then_inc(ld_tok, 16)
            eng.dma_start(proj_s[0:RANK, :], proj).then_inc(ld_att, 16)
            eng.dma_start(proj_s[RANK:P, :], proj).then_inc(ld_att, 16)
            eng.dma_start(lnw_s[:, :], ln_w).then_inc(ld_att, 16)
            eng.dma_start(lnb_s[:, :], ln_b).then_inc(ld_att, 16)
            eng.dma_start(wqk_s[:, :, 0:D], wq).then_inc(ld_att, 16)
            eng.dma_start(wqk_s[:, :, D:2 * D], wk).then_inc(ld_att, 16)
            eng.dma_start(wv_s[:, :, :], wv).then_inc(ld_att, 16)
            eng.dma_start(wo_s[:, :, :], wo).then_inc(ld_att, 16)
            eng.dma_start(rw_s[:, :, :], router).then_inc(ld_att, 16)
            for e in range(EXPERTS):
                eng.dma_start(gu_s[:, e], gate_up[:, e]).then_inc(ld_gu, 16)

            def store(at):
                eng.wait_ge(x2_sb, at.i + 1)
                eng.dma_start(xs[bass.ds(at.i * SEQ, SEQ), :], x2[:, at.u, :]).then_inc(x2_out[at.u], 16)

            with eng.Fori(0, SEQS // 2) as k:
                store(At(k, 0))
                store(At(k, 1))

            eng.wait_ge(routed, 3)
            for e in range(EXPERTS):
                eng.dma_start(down_s[:, e], down[:, e]).then_inc(ld_down, 16)

            for u in range(2):
                eng.wait_ge(y_out[u], 16 * ((TILES + 1 - u) // 2))

            def comb_load(m, u, free):
                wait(eng, comb_b, free)
                eng.dma_start(xe_t[:, u].rearrange("p a b -> p (a b)"), ys[bass.ds(m * 2 * P, P), :]).then_inc(comb_in[u], 16)
                eng.dma_start(y_s[:, u, :], ys[bass.ds((m * 2 + 1) * P, P), :]).then_inc(comb_in[u], 16)

            def comb_store(m, u):
                eng.wait_ge(comb_b, m + 1)
                eng.dma_start(out[m], hidden[:, m, :]).then_inc(fin[u], 16)

            comb_load(0, 0, 0)
            comb_load(1, 1, 0)
            with eng.Fori(0, SEQS // 2 - 1) as k:
                for u in range(2):
                    comb_store(2 * k + u, u)
                    comb_load(2 * k + u + 2, u, 2 * k + u + 1)
            for u in range(2):
                comb_store(SEQS - 2 + u, u)
            for u in range(2):
                eng.wait_ge(fin[u], 16 * (SEQS // 2))

        @block.gpsimd
        def _(eng):
            eng.memset(ident[:, :], 0.0).then_inc(const_p, 1)
            eng.memset(headmask[:, :], 1.0).then_inc(const_p, 1)
            eng.memset(causal[:, :], 0.0).then_inc(const_p, 1)
            eng.memset(before[:, :], 1.0).then_inc(const_p, 1)
            eng.memset(minus_half[:, :], -0.5).then_inc(const_p, 1)
            eng.iota(tok_of[:, :], pattern=[[P, TILES]], base=TRASH + 1, channel_multiplier=1).then_inc(const_p, 1)
            eng.iota(row_of[:, :], pattern=[[1, TILES]], base=0, channel_multiplier=0).then_inc(const_p, 1)
            eng.iota(region[:, 0:P].bitcast(I32), pattern=[[1, P]], base=0, channel_multiplier=0).then_inc(const_p, 1)
            eng.iota(region[:, P:P + 1].bitcast(I32), pattern=[[1, 1]], base=1, channel_multiplier=1).then_inc(const_p, 1)
            eng.iota(region[:, 2 * P:2 * P + EXPERTS].bitcast(I32), pattern=[[-1, EXPERTS]], base=EXPERTS, channel_multiplier=0).then_inc(const_p, 1)
            eng.wait_ge(const_p, 10)
            eng.affine_select(out=ident[:, :], in_=ident[:, :], compare_op=ALU.not_equal, fill=1.0, base=0,
                              pattern=[[-1, P]], channel_multiplier=1).then_inc(const_q, 1)
            eng.affine_select(out=causal[:, :], in_=causal[:, :], compare_op=ALU.is_ge, fill=NEG, base=0,
                              pattern=[[0, QH], [-1, P]], channel_multiplier=1).then_inc(const_q, 1)
            eng.affine_select(out=before[:, :], in_=before[:, :], compare_op=ALU.is_gt, fill=0.0, base=0,
                              pattern=[[1, P]], channel_multiplier=-1).then_inc(const_q, 1)
            eng.affine_select(out=headmask[:, :], in_=headmask[:, :], compare_op=ALU.is_ge, fill=0.0, base=0,
                              pattern=[[-HD, 8]], channel_multiplier=1).then_inc(const_q, 1)
            eng.wait_ge(const_q, 4)
            eng.affine_select(out=headmask[:, :], in_=headmask[:, :], compare_op=ALU.is_ge, fill=0.0, base=HD - 1,
                              pattern=[[HD, 8]], channel_multiplier=-1).then_inc(const_q, 1)
            eng.wait_ge(hashed, 5)

            def gather(at):
                wait(eng, embT_ps, at.i - 1)
                eng.tensor_copy(gathered_idx[:, at.u, :], hash_s[:, at.i, :]).then_inc(idx_ready, 1)
                wait_apart(eng, idx_ready, at.i + 1, (hashed, 5))
                for c in range(2):
                    eng.indirect_dma_start(
                        out=pair_emb[:, at.u, c * RANK:(c + 1) * RANK], out_offset=None, in_=emb,
                        in_offset=bass.IndirectOffsetOnAxis(ap=gathered_idx[:, at.u, c:c + 1], axis=0),
                    ).then_inc(emb_in[at.u], 16)

            gather(At(0, 0))
            last_front = SEQS - 1

            def step(front, mid, back):
                if front is not None and not (isinstance(front.i, int) and front.i == last_front):
                    gather(front.plus(1))
                if front is not None:
                    eng.wait_ge(f_a, front.i + 1)
                    eng.tensor_tensor(rF[:, :], aF[:, :], minus_half[:, :], ALU.pow).then_inc(f_pow, 1)
                if back is not None:
                    eng.wait_ge(o_a, back.i + 1)
                    eng.tensor_tensor(rO[:, 0:1], aO[:, 0:1], minus_half[:, 0:1], ALU.pow).then_inc(o_pow, 1)

            run_sequences(eng, step)

            def weigh(g, u):
                wait_apart(eng, oh_hi, g + 1, (hashed, 5))
                if not isinstance(g, int):
                    wait_apart(eng, tab_mm, g - 1, (hashed, 5))
                hi = onehot_hi[:, u, 0:GROUP * TILES].rearrange("p (c t) -> p c t", c=GROUP)
                hv = onehot_hv[:, u, 0:2 * GROUP * TILES].rearrange("p (c v t) -> p c v t", c=GROUP, v=2)
                eng.tensor_scalar(hv[:, :, 0, :], hi, place1[:, 0:1], None, ALU.mult).then_inc(oh_hp, 1)
                eng.tensor_tensor(hv[:, :, 1, :], hi,
                                  iota_pair[:, bass.ds(g * GROUP, GROUP)].unsqueeze(2).to_broadcast([P, GROUP, TILES]),
                                  ALU.mult).then_inc(oh_hc, 1)

            weigh(0, 0)
            weigh(1, 1)
            with eng.Fori(1, PAIRS // GROUP // 2) as k:
                weigh(2 * k, 0)
                weigh(2 * k + 1, 1)

            eng.wait_ge(routed, 3)
            for u in range(2):
                eng.wait_ge(x2_out[u], 16 * (SEQS // 2))

            def fetch(at):
                wait(eng, xeT_ps, at.i - 1)
                eng.tensor_copy(tok_idx[:, at.u:at.u + 1], tok_of[:, bass.ds(at.i, 1)]).then_inc(tidx, 1)
                wait_apart(eng, tidx, at.i + 1, (routed, 3))
                eng.indirect_dma_start(
                    out=xe[:, at.u, :], out_offset=None, in_=xs,
                    in_offset=bass.IndirectOffsetOnAxis(ap=tok_idx[:, at.u:at.u + 1], axis=0),
                ).then_inc(xe_in[at.u], 16)

            def scatter(at):
                wait(eng, y_out[at.u], 16 * at.k)
                eng.tensor_copy(row_idx[:, at.u:at.u + 1], row_of[:, bass.ds(at.i, 1)]).then_inc(ridx, 1)
                wait_apart(eng, ridx, at.i + 1, (routed, 3))
                eng.wait_ge(y_sb, at.i + 1)
                eng.indirect_dma_start(
                    out=ys, out_offset=bass.IndirectOffsetOnAxis(ap=row_idx[:, at.u:at.u + 1], axis=0),
                    in_=y_s[:, at.u, :], in_offset=None,
                ).then_inc(y_out[at.u], 16)

            fetch(At(0, 0))
            fetch(At(0, 1))
            fetch(At(1, 0))
            scatter(At(0, 0))
            fetch(At(1, 1))
            scatter(At(0, 1))
            with eng.Fori(1, (TILES - 3) // 2) as k:
                for u in range(2):
                    fetch(At(k, u).plus(2))
                    scatter(At(k, u))
            for i in range(2 * ((TILES - 3) // 2), TILES):
                if i + 2 < TILES:
                    fetch(At((i + 2) // 2, i % 2))
                scatter(At(i // 2, i % 2))

        @block.tensor
        def _(eng):
            eng.wait_ge(const_q, 5)
            eng.wait_ge(const_v, N_EXP_CONST)
            eng.wait_ge(ld_att, N_ATT)

            def scores(at, q):
                n = 4 * at.i + q
                if q == 0:
                    eng.wait_ge(k_sb, at.i + 1)
                eng.wait_ge(q_sb, n + 1)
                wait(eng, shift_sb, n - 1)
                s = S[q % 2]
                eng.matmul(s[:, :], identb[:, :], causal[:, :], start=True, stop=False)
                for h in range(QH):
                    mm = eng.matmul(s[:, h * P:(h + 1) * P], q_masked[:, q * QH + h, :], k_t[:, at.u, q // 2, :],
                                    start=False, stop=(h == QH - 1))
                mm.then_inc(s_ps, 1)

            def probs_turn(at, q):
                n = 4 * at.i + q
                eng.wait_ge(exp_sb, n + 1)
                wait(eng, pT_sb, n - 1)
                for h in range(QH):
                    mm = eng.transpose(PT[q % 2][:, h * P:(h + 1) * P], probs[:, q % 2, h * P:(h + 1) * P], ident[:, :])
                mm.then_inc(pT_ps, 1)

            def weigh_values(at, q):
                n = 4 * at.i + q
                eng.wait_ge(pT_sb, n + 1)
                if q == 0:
                    eng.wait_ge(v_sb, at.i + 1)
                    wait(eng, attn_sb, at.i)
                for h in range(QH):
                    c = (q * QH + h) * VW
                    mm = eng.matmul(AV[:, c:c + AVN], probs_t[:, q % 2, h * P:(h + 1) * P], v_one[:, at.u, c:c + AVN],
                                    start=True, stop=True)
                mm.then_inc(av_ps, 1)

            def turn(dst, src, done):
                for c in range(KC):
                    mm = eng.transpose(dst[:, c * P:(c + 1) * P], src[:, c * P:(c + 1) * P], ident[:, :])
                mm.then_inc(done, 1)

            def step(front, mid, back):
                if mid is not None:
                    scores(mid, 0)
                if front is not None:
                    eng.wait_ge(emb_in[front.u], 32 * (front.k + 1))
                    wait(eng, q_sb, 4 * front.i)
                    wait(eng, k_sb, front.i)
                    eng.transpose(FB[:, 0:P], pair_emb[:, front.u, :], ident[:, :]).then_inc(embT_ps, 1)
                if back is not None:
                    eng.wait_ge(attn_sb, back.i + 1)
                    wait(eng, lg_sb, back.i)
                    turn(OB, attn, attnT_ps)
                if mid is not None:
                    scores(mid, 1)
                if front is not None:
                    eng.wait_ge(embT_sb, front.i + 1)
                    eng.matmul(FB[:, P:P + D], emb_t[:, :], proj_s[:, :], start=True, stop=True).then_inc(h_ps, 1)
                if back is not None:
                    eng.wait_ge(attnT_sb, back.i + 1)
                    for c in range(KC):
                        mm = eng.matmul(OB[:, D:2 * D], attn_t[:, c, :], wo_s[:, c, :], start=(c == 0), stop=(c == KC - 1))
                    mm.then_inc(o_ps, 1)
                if mid is not None:
                    probs_turn(mid, 0)
                    scores(mid, 2)
                    weigh_values(mid, 0)
                    probs_turn(mid, 1)
                if front is not None:
                    eng.wait_ge(z_sb, front.i + 1)
                    eng.wait_ge(base_sb, front.i + 1)
                    turn(FB, z, zT_ps)
                if mid is not None:
                    scores(mid, 3)
                    weigh_values(mid, 1)
                if back is not None:
                    eng.wait_ge(x2_sb, back.i + 1)
                    turn(OB, x2[:, back.u, :], x2T_ps)
                if front is not None:
                    eng.wait_ge(yT_sb, front.i + 1)
                    for m in range(4):
                        for c in range(KC):
                            mm = eng.matmul(FB[:, m * P:(m + 1) * P], wqk_s[:, c, m * P:(m + 1) * P], y_t[:, c, :],
                                            start=(c == 0), stop=(c == KC - 1))
                    mm.then_inc(qk_ps, 1)
                if mid is not None:
                    probs_turn(mid, 2)
                    weigh_values(mid, 2)
                if front is not None:
                    wait(eng, v_sb, front.i)
                    for c in range(KC):
                        mm = eng.matmul(VB[:, 0:D], y_t[:, c, :], wv_s[:, c, :], start=(c == 0), stop=(c == KC - 1))
                    mm.then_inc(v_ps, 1)
                if back is not None:
                    eng.wait_ge(x2T_sb, back.i + 1)
                    for c in range(KC):
                        mm = eng.matmul(OB[:, D:D + RN], x2_t[:, c, :], rw_s[:, c, :], start=(c == 0), stop=(c == KC - 1))
                    mm.then_inc(lg_ps, 1)
                if mid is not None:
                    probs_turn(mid, 3)
                    weigh_values(mid, 3)

            run_sequences(eng, step)

            eng.wait_ge(counted, 1)
            bh = both_h.rearrange("p a b -> p (a b)")
            eng.matmul(bank[0][:, 0:NE], before[:, :], bh, start=True, stop=False)
            eng.matmul(bank[0][:, 0:NE], onesb[:, :], cum_h[:, 0:SEQS, :].rearrange("p a b -> p (a b)"), start=False, stop=True).then_inc(rank_ps, 1)
            eng.matmul(bank[1][:, 0:EXPERTS], onesb[:, :], cum_h[:, SEQS, :], start=True, stop=True).then_inc(rank_ps, 1)

            def fill(g, u, first=False, last=False):
                eng.wait_ge(oh_lo, g + 1)
                eng.wait_ge(oh_hp, g + 1)
                eng.wait_ge(oh_hc, g + 1)
                for c in range(GROUP):
                    mm = eng.matmul(bank[2][:, 0:2 * TILES], onehot_lo[:, u, c * P:(c + 1) * P],
                                    onehot_hv[:, u, c * 2 * TILES:(c + 1) * 2 * TILES],
                                    start=(first and c == 0), stop=(last and c == GROUP - 1))
                mm.then_inc(tab_mm, 1)

            groups = PAIRS // GROUP
            fill(0, 0, first=True)
            fill(1, 1)
            with eng.Fori(1, groups // 2 - 1) as k:
                fill(2 * k, 0)
                fill(2 * k + 1, 1)
            fill(groups - 2, 0)
            fill(groups - 1, 1, last=True)

            eng.wait_ge(routed, 3)
            eng.wait_ge(ld_gu, 16 * EXPERTS)

            def tokens_turn(at):
                eng.wait_ge(xe_in[at.u], 16 * (at.k + 1))
                wait(eng, xeT_sb, at.i)
                turn(bank[7], xe[:, at.u, :], xeT_ps)

            def widen(at, e, half):
                if half == 0:
                    eng.wait_ge(xeT_sb, at.i + 1)
                wait(eng, hid2_sb, 2 * at.i + half - 1)
                for g in range(2):
                    for c in range(KC):
                        mm = eng.matmul(bank[2 * half + g][:, 0:HALF], xe_t[:, at.u, c, :], gu_s[:, e, c, half, g, :],
                                        start=(c == 0), stop=(c == KC - 1))
                mm.then_inc(gu_ps, 1)

            def inner_turn(at, half):
                n = 2 * at.i + half
                eng.wait_ge(hid2_sb, n + 1)
                wait(eng, hT_sb, n - 1)
                for c, w in enumerate(CHUNKS):
                    mm = eng.transpose(bank[4 + half][0:w, c * P:(c + 1) * P], h_s[:, half, c * P:c * P + w], ident[:, :])
                mm.then_inc(hT_ps, 1)

            def narrow(at, e):
                eng.wait_ge(hT_sb, 2 * at.i + 2)
                wait(eng, y_sb, at.i)
                for half in range(2):
                    for c, w in enumerate(CHUNKS):
                        mm = eng.matmul(bank[6][:, 0:D], h_t[0:w, half, c, :], down_s[0:w, e, 3 * half + c, :],
                                        start=(half == 0 and c == 0), stop=(half == 1 and c == 2))
                mm.then_inc(y_ps, 1)

            def expert_of(at):
                return eng.value_load(exp_of[0:1, bass.ds(at.i, 1)], min_val=0, max_val=EXPERTS - 1)

            def tile(at, prev, nxt, e_prev):
                e = expert_of(at)
                widen(at, e, 0)
                widen(at, e, 1)
                if prev is not None:
                    narrow(prev, e_prev)
                if nxt is not None:
                    tokens_turn(nxt)
                inner_turn(at, 0)
                inner_turn(at, 1)
                return e

            tokens_turn(At(0, 0))
            e = tile(At(0, 0), None, At(0, 1), None)
            eng.wait_ge(ld_down, 16 * EXPERTS)
            with eng.Fori(0, (TILES - 3) // 2) as k:
                a, b = At(k, 0), At(k, 1)
                e_b = tile(b, a, b.plus(1), expert_of(a))
                tile(a.plus(2), b, b.plus(2), e_b)
            a, b = At((TILES - 3) // 2, 0), At((TILES - 3) // 2, 1)
            e_b = tile(b, a, b.plus(1), expert_of(a))
            tile(b.plus(1), b, None, e_b)
            narrow(At(TILES // 2, 0), expert_of(At(TILES // 2, 0)))

        @block.scalar
        def _(eng):
            eng.wait_ge(ld_att, N_ATT)

            def exps(at, q):
                n = 4 * at.i + q
                eng.wait_ge(shift_sb, n + 1)
                wait(eng, pT_ps, n - 1)
                eng.activation(probs[:, q % 2, :], shifted[:, q % 2, :], ACT.Exp, scale=SCALE).then_inc(exp_sb, 1)

            def probs_copy(at, q):
                n = 4 * at.i + q
                eng.wait_ge(pT_ps, n + 1)
                wait(eng, av_ps, n - 1)
                eng.copy(probs_t[:, q % 2, :], PT[q % 2][:, :]).then_inc(pT_sb, 1)

            def step(front, mid, back):
                if front is not None:
                    eng.wait_ge(embT_ps, front.i + 1)
                    wait(eng, h_ps, front.i)
                    eng.mul(emb_t[:, :], FB[:, 0:P], 0.5).then_inc(embT_sb, 1)
                if back is not None:
                    eng.wait_ge(attnT_ps, back.i + 1)
                    wait(eng, o_ps, back.i)
                    eng.copy(attn_t.rearrange("p a b -> p (a b)"), OB[:, 0:D]).then_inc(attnT_sb, 1)
                if mid is not None:
                    exps(mid, 0)
                    probs_copy(mid, 0)
                    exps(mid, 1)
                    probs_copy(mid, 1)
                if front is not None:
                    eng.wait_ge(zT_ps, front.i + 1)
                    wait(eng, v_ps, front.i)
                    for c in range(KC):
                        act = eng.activation(y_t[:, c, :], FB[:, c * P:(c + 1) * P], ACT.Identity,
                                             bias=lnb_s[:, c:c + 1], scale=lnw_s[:, c:c + 1])
                    act.then_inc(yT_sb, 1)
                if back is not None:
                    eng.wait_ge(x2T_ps, back.i + 1)
                    wait(eng, lg_ps, back.i)
                    eng.copy(x2_t.rearrange("p a b -> p (a b)"), OB[:, 0:D]).then_inc(x2T_sb, 1)
                if mid is not None:
                    exps(mid, 2)
                if front is not None:
                    eng.wait_ge(qk_ps, front.i + 1)
                    wait(eng, s_ps, 4 * front.i - 4)
                    eng.copy(k_t[:, front.u].rearrange("p a b -> p (a b)"), FB[:, 2 * P:4 * P]).then_inc(k_sb, 1)
                if mid is not None:
                    probs_copy(mid, 2)
                if front is not None:
                    eng.wait_ge(v_ps, front.i + 1)
                    wait(eng, av_ps, 4 * front.i - 4)
                    eng.copy(v_one[:, front.u, 0:HEADS * VW].rearrange("p (h v) -> p h v", v=VW)[:, :, 0:HD],
                             VB[:, 0:D].rearrange("p (h v) -> p h v", v=HD)).then_inc(v_sb, 1)
                if mid is not None:
                    exps(mid, 3)
                    probs_copy(mid, 3)

            run_sequences(eng, step)

            eng.wait_ge(wexp_in, 2)
            eng.activation(lg2.rearrange("p a b -> p (a b)"), work_b.rearrange("p a b -> p (a b)"), ACT.Exp).then_inc(wexp, 1)
            eng.activation(top_w[:, 1, :], top2, ACT.Exp).then_inc(wexp, 1)

            def tile(at, nxt):
                for half in range(2):
                    n = 2 * at.i + half
                    eng.wait_ge(gu_ps, n + 1)
                    wait(eng, hid2_sb, n - 1)
                    eng.activation(silu[:, half, :], bank[2 * half][:, 0:HALF], ACT.Silu).then_inc(silu_sb, 1)
                if nxt is not None:
                    eng.wait_ge(xeT_ps, nxt.i + 1)
                    wait(eng, gu_ps, 2 * nxt.i - 2)
                    eng.copy(xe_t[:, nxt.u].rearrange("p a b -> p (a b)"), bank[7][:, 0:D]).then_inc(xeT_sb, 1)
                for half in range(2):
                    n = 2 * at.i + half
                    eng.wait_ge(hT_ps, n + 1)
                    wait(eng, y_ps, at.i)
                    eng.copy(h_t[:, half, 0:2].rearrange("p a b -> p (a b)"), bank[4 + half][:, 0:2 * P])
                    eng.copy(h_t[0:CHUNKS[2], half, 2], bank[4 + half][0:CHUNKS[2], 2 * P:3 * P]).then_inc(hT_sb, 1)

            eng.wait_ge(xeT_ps, 1)
            eng.copy(xe_t[:, 0].rearrange("p a b -> p (a b)"), bank[7][:, 0:D]).then_inc(xeT_sb, 1)
            tile(At(0, 0), At(0, 1))
            with eng.Fori(0, (TILES - 3) // 2) as k:
                tile(At(k, 1), At(k, 0).plus(2))
                tile(At(k, 0).plus(2), At(k, 1).plus(2))
            tile(At((TILES - 3) // 2, 1), At((TILES - 1) // 2, 0))
            tile(At((TILES - 1) // 2, 0), None)

        @block.vector
        def _(eng):
            eng.memset(onesb[:, :], 1.0).then_inc(const_v, 1)
            eng.memset(ln_mul[:, 0:1], 1.0).then_inc(const_v, 1)
            eng.memset(ln_mul[:, 1:2], 1.0 + EPS).then_inc(const_v, 1)
            eng.memset(ln_add[:, 0:1], EPS).then_inc(const_v, 1)
            eng.memset(ln_add[:, 1:2], EPS * EPS).then_inc(const_v, 1)
            eng.wait_ge(const_p, 10)
            eng.tensor_copy(iota_trash[:, :], tok_of[:, :]).then_inc(const_v, 1)
            eng.tensor_copy(iota_tile[:, :], row_of[:, :]).then_inc(const_v, 1)
            eng.tensor_copy(iota_lo[:, :], region[:, 0:P].bitcast(I32)).then_inc(const_v, 1)
            eng.tensor_copy(place1[:, :], region[:, P:P + 1].bitcast(I32)).then_inc(const_v, 1)
            eng.tensor_copy(low_first[:, :], region[:, 2 * P:2 * P + EXPERTS].bitcast(I32)).then_inc(const_v, 1)
            eng.wait_ge(const_q, 1)
            eng.tensor_copy(identb[:, :], ident[:, :]).then_inc(const_v, 1)
            eng.wait_ge(const_v, 11)
            eng.tensor_copy(iota_pair[:, :], iota_lo[:, 0:PAIRS])
            eng.memset(v_one.rearrange("p a b -> p (a b)"), 1.0).then_inc(const_v, 1)

            eng.wait_ge(ld_tok, 16)
            eng.tensor_scalar(tok_s[:, :], tok_s[:, :], BUCKETS - 1, None, ALU.bitwise_and).then_inc(hashed, 1)
            eng.wait_ge(hashed, 1)
            eng.tensor_scalar(hash_s[:, :, 0], tok_s[:, :], 31.0, 7.0, ALU.mult, ALU.add).then_inc(hashed, 1)
            eng.tensor_scalar(hash_s[:, :, 1], tok_s[:, :], 131.0, 13.0, ALU.mult, ALU.add).then_inc(hashed, 1)
            eng.wait_ge(hashed, 3)
            for c in range(2):
                eng.tensor_scalar(hash_s[:, :, c], hash_s[:, :, c], BUCKETS - 1, None, ALU.bitwise_and).then_inc(hashed, 1)

            def softmax_shift(at, q):
                n = 4 * at.i + q
                s = S[q % 2][:, :].rearrange("p (h t) -> p h t", h=QH)
                eng.wait_ge(s_ps, n + 1)
                eng.tensor_reduce(rowmax[:, q % 2, :], s, AX, ALU.max).then_inc(max_sb, 1)
                eng.wait_ge(max_sb, n + 1)
                wait(eng, exp_sb, n - 1)
                eng.tensor_tensor(shifted[:, q % 2, :].rearrange("p (h t) -> p h t", h=QH), s,
                                  rowmax[:, q % 2, :].unsqueeze(2).to_broadcast([P, QH, P]), ALU.subtract).then_inc(shift_sb, 1)

            def queries(front, q):
                if q == 0:
                    eng.wait_ge(k_sb, front.i + 1)
                wait(eng, s_ps, 4 * front.i + q - 3)
                g = q // 2
                eng.tensor_tensor(q_masked[:, q * QH:(q + 1) * QH, :],
                                  FB[:, g * P:(g + 1) * P].unsqueeze(1).to_broadcast([P, QH, P]),
                                  headmask[:, (q % 2) * QH:(q % 2 + 1) * QH].unsqueeze(2).to_broadcast([P, QH, P]),
                                  ALU.mult).then_inc(q_sb, 1)

            def step(front, mid, back):
                if back is not None:
                    eng.wait_ge(av_ps, 4 * back.i + 4)
                    o = AV[:, 0:HEADS * VW].rearrange("p (h v) -> p h v", v=VW)
                    eng.reciprocal(recip[:, :], o[:, :, HD]).then_inc(rec_sb, 1)
                    eng.wait_ge(rec_sb, back.i + 1)
                    wait(eng, attnT_ps, back.i)
                    eng.tensor_tensor(attn.rearrange("p (h v) -> p h v", v=HD), o[:, :, 0:HD],
                                      recip.unsqueeze(2).to_broadcast([P, HEADS, HD]), ALU.mult).then_inc(attn_sb, 1)
                if mid is not None:
                    softmax_shift(mid, 0)
                if front is not None:
                    wait_apart(eng, h_ps, front.i + 1, (hashed, 5))
                    h = FB[:, P:P + D]
                    eng.bn_stats(bnF[:, :], h).then_inc(f_bn, 1)
                    wait_apart(eng, f_bn, front.i + 1, (hashed, 5))
                    eng.bn_aggr(mvF[:, :], bnF[:, :]).then_inc(f_mv, 1)
                    eng.wait_ge(f_mv, front.i + 1)
                    eng.scalar_tensor_tensor(out=aF[:, :], in0=ln_mul[:, :], scalar=mvF[:, 1:2], in1=ln_add[:, :],
                                             op0=ALU.mult, op1=ALU.add).then_inc(f_a, 1)
                if mid is not None:
                    softmax_shift(mid, 1)
                if front is not None:
                    eng.wait_ge(f_pow, front.i + 1)
                    eng.tensor_scalar(nmF[:, :], rF[:, :], mvF[:, 0:1], -1.0, ALU.mult, ALU.mult).then_inc(f_nm, 1)
                    eng.tensor_scalar(aF[:, 0:1], rF[:, 0:1], 1.0, None, ALU.add).then_inc(f_r1, 1)
                    eng.wait_ge(f_nm, front.i + 1)
                    wait(eng, zT_ps, front.i)
                    eng.tensor_scalar(z[:, :], h, rF[:, 1:2], nmF[:, 1:2], ALU.mult, ALU.add).then_inc(z_sb, 1)
                    eng.wait_ge(f_r1, front.i + 1)
                    eng.tensor_scalar(hidden[:, front.i, :], h, aF[:, 0:1], nmF[:, 0:1], ALU.mult, ALU.add).then_inc(base_sb, 1)
                if back is not None:
                    eng.wait_ge(o_ps, back.i + 1)
                    eng.tensor_tensor(hidden[:, back.i, :], OB[:, D:2 * D], hidden[:, back.i, :], ALU.add).then_inc(hid_sb, 1)
                    wait_apart(eng, hid_sb, back.i + 1, (hashed, 5))
                    eng.bn_stats(bnO[:, :], hidden[:, back.i, :]).then_inc(o_bn, 1)
                    wait_apart(eng, o_bn, back.i + 1, (hashed, 5))
                    eng.bn_aggr(mvO[:, :], bnO[:, :]).then_inc(o_mv, 1)
                    eng.wait_ge(o_mv, back.i + 1)
                    eng.tensor_scalar(aO[:, 0:1], mvO[:, 1:2], EPS, None, ALU.add).then_inc(o_a, 1)
                if mid is not None:
                    softmax_shift(mid, 2)
                if back is not None:
                    eng.wait_ge(o_pow, back.i + 1)
                    eng.tensor_scalar(nmO[:, 0:1], rO[:, 0:1], mvO[:, 0:1], -1.0, ALU.mult, ALU.mult).then_inc(o_nm, 1)
                    eng.wait_ge(o_nm, back.i + 1)
                    wait(eng, x2T_ps, back.i - 1)
                    wait(eng, x2_out[back.u], 16 * back.k)
                    eng.tensor_scalar(x2[:, back.u, :], hidden[:, back.i, :], rO[:, 0:1], nmO[:, 0:1], ALU.mult,
                                      ALU.add).then_inc(x2_sb, 1)
                if front is not None:
                    queries(front, 0)
                    queries(front, 1)
                if mid is not None:
                    softmax_shift(mid, 3)
                if front is not None:
                    queries(front, 2)
                    queries(front, 3)
                if back is not None:
                    eng.wait_ge(lg_ps, back.i + 1)
                    eng.tensor_copy(logits[:, back.i, :], OB[:, D:D + EXPERTS]).then_inc(lg_sb, 1)

            run_sequences(eng, step)

            steps = [0]

            def done(instruction):
                steps[0] += 1
                instruction.then_inc(route, 1)
                eng.wait_ge(route, steps[0])

            def wide(a, n=EXPERTS):
                return a.unsqueeze(2).to_broadcast([P, SEQS, n])

            first = low_first[:, :].unsqueeze(1).to_broadcast([P, SEQS, EXPERTS])
            eng.wait_ge(lg_sb, SEQS)
            done(eng.tensor_reduce(top1, logits[:, :, :], AX, ALU.max))
            done(eng.tensor_tensor(work_a, logits[:, :, :], wide(top1), ALU.is_equal))
            done(eng.tensor_tensor(work_a, work_a, first, ALU.mult))
            done(eng.tensor_reduce(top2, work_a, AX, ALU.max))
            done(eng.tensor_tensor(rmask_a, work_a, wide(top2), ALU.is_equal))
            done(eng.scalar_tensor_tensor(out=lg2, in0=rmask_a, scalar=-3e38, in1=logits[:, :, :], op0=ALU.mult, op1=ALU.add))
            done(eng.tensor_reduce(esum[:, :], lg2, AX, ALU.max))
            done(eng.tensor_tensor(work_a, lg2, wide(esum[:, :]), ALU.is_equal))
            done(eng.tensor_tensor(work_a, work_a, first, ALU.mult))
            done(eng.tensor_reduce(top2, work_a, AX, ALU.max))
            done(eng.tensor_tensor(rmask_b, work_a, wide(top2), ALU.is_equal))
            eng.tensor_tensor(work_b, logits[:, :, :], wide(top1), ALU.subtract).then_inc(wexp_in, 1)
            eng.tensor_tensor(top2, esum[:, :], top1, ALU.subtract).then_inc(wexp_in, 1)
            done(eng.tensor_tensor(cum_a, rmask_a, rmask_b, ALU.add))
            src, dst, shift = cum_a, cum_b, 1
            while shift < SEQS:
                steps[0] += 2
                eng.tensor_copy(dst[:, 0:shift, :], src[:, 0:shift, :]).then_inc(route, 1)
                eng.tensor_tensor(dst[:, shift:, :], src[:, shift:, :], src[:, 0:SEQS - shift, :], ALU.add).then_inc(route, 1)
                eng.wait_ge(route, steps[0])
                src, dst, shift = dst, src, 2 * shift
            done(eng.memset(cum_h[:, 0, :], 0.0))
            done(eng.tensor_copy(cum_h[:, 1:, :], src))
            eng.tensor_tensor(both_h, rmask_a, rmask_b, ALU.add).then_inc(counted, 1)
            eng.wait_ge(rank_ps, 2)
            done(eng.tensor_scalar(count_i, bank[1][:, 0:EXPERTS], float(P - 1), None, ALU.add))
            done(eng.tensor_scalar(tiles_i, count_i, 7, None, ALU.arith_shift_right))
            done(eng.tensor_copy(tiles_f, tiles_i))
            a, b, shift = tiles_f, ends, 1
            for shift, a, b in ((1, tiles_f, ends), (2, ends, ends2), (4, ends2, ends)):
                steps[0] += 2
                eng.tensor_copy(b[:, 0:shift], a[:, 0:shift]).then_inc(route, 1)
                eng.tensor_tensor(b[:, shift:], a[:, shift:], a[:, 0:EXPERTS - shift], ALU.add).then_inc(route, 1)
                eng.wait_ge(route, steps[0])
            done(eng.tensor_tensor(base, ends, tiles_f, ALU.subtract))
            done(eng.tensor_scalar(base, base, float(P), None, ALU.mult))
            done(eng.tensor_tensor(work_a, bank[0][:, 0:NE].rearrange("p (a b) -> p a b", b=EXPERTS),
                                   base.unsqueeze(1).to_broadcast([P, SEQS, EXPERTS]), ALU.add))
            for c, m in enumerate((rmask_a, rmask_b)):
                done(eng.tensor_tensor(cum_a, work_a, m, ALU.mult))
                done(eng.tensor_reduce(pos_f[:, :, c], cum_a, AX, ALU.add))
            done(eng.tensor_copy(pos_i, pos_f))
            done(eng.tensor_scalar(hi_i, pos_i, 7, None, ALU.arith_shift_right))
            done(eng.tensor_scalar(lo_i, pos_i, P - 1, None, ALU.bitwise_and))
            done(eng.tensor_copy(hi_f, hi_i))
            done(eng.tensor_copy(lo_f, lo_i))

            def onehots(g, u):
                wait(eng, tab_mm, g - 1)
                lo = lo_f.rearrange("p a b -> p (a b)")[:, bass.ds(g * GROUP, GROUP)]
                hi = hi_f.rearrange("p a b -> p (a b)")[:, bass.ds(g * GROUP, GROUP)]
                eng.tensor_tensor(onehot_lo[:, u, :].rearrange("p (c t) -> p c t", c=GROUP),
                                  iota_lo[:, :].unsqueeze(1).to_broadcast([P, GROUP, P]),
                                  lo.unsqueeze(2).to_broadcast([P, GROUP, P]), ALU.is_equal).then_inc(oh_lo, 1)
                wait(eng, oh_hc, g - 1)
                eng.tensor_tensor(onehot_hi[:, u, 0:GROUP * TILES].rearrange("p (c t) -> p c t", c=GROUP),
                                  iota_tile[:, :].unsqueeze(1).to_broadcast([P, GROUP, TILES]),
                                  hi.unsqueeze(2).to_broadcast([P, GROUP, TILES]), ALU.is_equal).then_inc(oh_hi, 1)

            onehots(0, 0)
            onehots(1, 1)
            with eng.Fori(1, PAIRS // GROUP // 2) as k:
                onehots(2 * k, 0)
                onehots(2 * k + 1, 1)

            eng.wait_ge(wexp, 2)
            done(eng.tensor_reduce(esum[:, :], lg2, AX, ALU.add))
            done(eng.reciprocal(top_w[:, 0, :], esum[:, :]))
            done(eng.tensor_tensor(top_w[:, 1, :], top_w[:, 1, :], top_w[:, 0, :], ALU.mult))
            done(eng.tensor_tensor(cmp_f, iota_tile[:, :].unsqueeze(2).to_broadcast([P, TILES, EXPERTS]),
                                   ends.unsqueeze(1).to_broadcast([P, TILES, EXPERTS]), ALU.is_ge))
            done(eng.tensor_reduce(exp_f, cmp_f, AX, ALU.add))
            eng.tensor_scalar(exp_of[:, :], exp_f[0:1, :], float(EXPERTS - 1), None, ALU.min).then_inc(routed, 1)
            eng.wait_ge(tab_mm, PAIRS // GROUP)
            done(eng.tensor_copy(tab.rearrange("p a b -> p (a b)"), bank[2][:, 0:2 * TILES]))
            place, pair = tab[:, 0, :], tab[:, 1, :]
            done(eng.tensor_scalar(empty, place, 0.0, None, ALU.is_equal))
            done(eng.tensor_tensor(place_f, empty, iota_trash[:, :], ALU.mult))
            done(eng.tensor_tensor(place_f, place_f, place, ALU.add))
            done(eng.scalar_tensor_tensor(out=place_f, in0=pair, scalar=float(P), in1=place_f, op0=ALU.mult, op1=ALU.add))
            eng.tensor_scalar(row_of[:, :], place_f, -1.0, None, ALU.add).then_inc(routed, 1)
            done(eng.tensor_copy(pair_i, pair))
            done(eng.tensor_scalar(half_i, pair_i, 1, None, ALU.arith_shift_right))
            done(eng.tensor_copy(half_f, half_i))
            done(eng.tensor_scalar(exp_f, place, -1.0, 0.0, ALU.add, ALU.max))
            eng.scalar_tensor_tensor(out=tok_of[:, :], in0=half_f, scalar=float(P), in1=exp_f, op0=ALU.mult,
                                     op1=ALU.add).then_inc(routed, 1)

            def product(at, half):
                n = 2 * at.i + half
                eng.wait_ge(silu_sb, n + 1)
                wait(eng, hT_ps, n - 1)
                eng.tensor_tensor(h_s[:, half, :], bank[2 * half + 1][:, 0:HALF], silu[:, half, :], ALU.mult).then_inc(hid2_sb, 1)

            def result(at):
                eng.wait_ge(y_ps, at.i + 1)
                wait(eng, y_out[at.u], 16 * at.k)
                eng.tensor_copy(y_s[:, at.u, :], bank[6][:, 0:D]).then_inc(y_sb, 1)

            def tile(at, prev):
                product(at, 0)
                product(at, 1)
                if prev is not None:
                    result(prev)

            tile(At(0, 0), None)
            with eng.Fori(0, (TILES - 1) // 2) as k:
                tile(At(k, 1), At(k, 0))
                tile(At(k, 0).plus(2), At(k, 1))
            result(At(TILES // 2, 0))

            def combine(m, u, n_in):
                eng.wait_ge(comb_in[u], n_in)
                eng.scalar_tensor_tensor(out=hidden[:, m, :], in0=xe_t[:, u].rearrange("p a b -> p (a b)"),
                                         scalar=top_w[:, 0, bass.ds(m, 1)], in1=hidden[:, m, :], op0=ALU.mult,
                                         op1=ALU.add).then_inc(comb_a, 1)
                eng.wait_ge(comb_a, m + 1)
                eng.scalar_tensor_tensor(out=hidden[:, m, :], in0=y_s[:, u, :], scalar=top_w[:, 1, bass.ds(m, 1)],
                                         in1=hidden[:, m, :], op0=ALU.mult, op1=ALU.add).then_inc(comb_b, 1)

            with eng.Fori(0, SEQS // 2) as k:
                for u in range(2):
                    combine(2 * k + u, u, 32 * (k + 1))


def kernel(x, L0_tok_weight, L0_tok_proj, L0_attn_ln_w, L0_attn_ln_b, L0_attn_wq, L0_attn_wk, L0_attn_wv,
           L0_attn_wo, L0_ffn_router_w, L0_ffn_gate_w, L0_ffn_up_w, L0_ffn_down_w):
    import numpy as np
    import concourse.bacc as bacc
    from concourse.bass_utils import run_bass_kernel_spmd

    def chunks(a):
        return np.asarray(a).reshape(KC, P, -1).transpose(1, 0, 2)

    def heads(a):
        return np.asarray(a).transpose(1, 0, 2).reshape(D, D)

    router = np.zeros((D, RN), np.float32)
    router[:, :EXPERTS] = np.asarray(L0_ffn_router_w).T
    gate, up = (np.asarray(w).reshape(EXPERTS, 2, HALF, KC, P).transpose(4, 0, 3, 1, 2)
                for w in (L0_ffn_gate_w, L0_ffn_up_w))
    gate_up = np.stack([gate, up], axis=4)
    by_inner = np.asarray(L0_ffn_down_w).transpose(0, 2, 1)
    down = np.zeros((P, EXPERTS, 6, D), np.float32)
    for half in range(2):
        for c, w in enumerate(CHUNKS):
            at = half * HALF + c * P
            down[:w, :, 3 * half + c] = by_inner[:, at:at + w].transpose(1, 0, 2)
    arrays = {
        "tokens": np.asarray(x).T, "emb": L0_tok_weight, "proj": L0_tok_proj,
        "ln_w": np.asarray(L0_attn_ln_w).reshape(KC, P).T, "ln_b": np.asarray(L0_attn_ln_b).reshape(KC, P).T,
        "wq": chunks(heads(L0_attn_wq)), "wk": chunks(heads(L0_attn_wk)), "wv": chunks(heads(L0_attn_wv)),
        "wo": chunks(L0_attn_wo), "router": chunks(router), "gate_up": gate_up, "down": down,
    }
    nc = bacc.Bacc("TRN2", target_bir_lowering=False, num_devices=1)
    ins, args = {}, []
    for name, a in arrays.items():
        ins["in_" + name] = np.ascontiguousarray(a)
        args.append(nc.dram_tensor("in_" + name, ins["in_" + name].shape,
                                   mybir.dt.from_np(ins["in_" + name].dtype), kind="ExternalInput").ap())
    out = nc.dram_tensor("out_hidden", (SEQS, SEQ, D), F32, kind="ExternalOutput").ap()
    build(nc, *args, out)
    return run_bass_kernel_spmd(nc, [ins], core_ids=[0]).results[0]["out_hidden"]
```

```python
from contextlib import ExitStack

import concourse.bass as bass
from concourse import mybir

F32 = mybir.dt.float32
BF16 = mybir.dt.bfloat16
I32 = mybir.dt.int32
U32 = mybir.dt.uint32
ALU = mybir.AluOpType
ACT = mybir.ActivationFunctionType
AX = mybir.AxisListType.X

P = 128
SEQS, SEQ = 32, 128
BUCKETS, RANK = 16384, 64
D, KC = 256, 2
HEADS, HD = 16, 16
EXPERTS, INNER = 8, 704
HALF = INNER // 2
CHUNKS = (128, 128, 96)
EPS = 1e-5
NEG = -1e30
QUARTERS, QH = 4, 4
VW = HD + 1
AVN = 96
RN = 96
PAIRS = 2 * SEQS
TILES = (2 * SEQS * SEQ + EXPERTS * (P - 1)) // P
TOKENS = SEQS * SEQ
XW = D + 2
GROUP = 8
DOWN_EARLY = 3
SCALE = HD ** -0.5


class At:

    def __init__(self, k, u):
        self.k, self.u = k, u
        self.i = 2 * k + u

    def plus(self, n):
        u = self.u + n
        return At(self.k + u // 2 if u // 2 else self.k, u % 2)


def wait(eng, sem, value):
    if isinstance(value, int) and value <= 0:
        return
    eng.wait_ge(sem, value)


def wait_apart(eng, sem, value, met):
    if not isinstance(value, int):
        value = eng.to_reg(value)
    eng.wait_ge(*met)
    eng.wait_ge(sem, value)


def build(nc, tokens, emb, proj, ln_w, ln_b, wq, wk, wv, wo, router, gate_up, down, out):
    xs = nc.dram_tensor("normed_tokens", (TOKENS, XW), F32).ap()

    ctx = ExitStack()
    with ctx:
        def sb(name, shape, dt=F32):
            return ctx.enter_context(nc.sbuf_tensor(name, shape, dt))

        def sem(name):
            return ctx.enter_context(nc.semaphore(name))

        bank = [ctx.enter_context(nc.psum_tensor(f"bank{n}", [P, 512], F32)) for n in range(8)]

        ident = sb("ident", [P, P])
        identb = sb("identb", [P, P], BF16)
        causal = sb("causal", [P, QH * P], BF16)
        headmask = sb("headmask", [P, 8])
        before = sb("before", [P, P], BF16)
        onesb = sb("onesb", [P, P], BF16)
        iota_lo = sb("iota_lo", [P, P])
        iota_tile = sb("iota_tile", [P, TILES])
        trash_row = sb("trash_row", [P, 1])
        iota_pair = sb("iota_pair", [P, PAIRS])
        place1 = sb("place1", [P, 1])
        iota_expert = sb("iota_expert", [P, EXPERTS])
        ln_mul = sb("ln_mul", [P, 2])
        ln_add = sb("ln_add", [P, 2])
        minus_half = sb("minus_half", [P, 2])

        proj_s = sb("proj_s", [P, D])
        wqk_s = sb("wqk_s", [P, KC, 2 * D])
        wv_s = sb("wv_s", [P, KC, D])
        wo_s = sb("wo_s", [P, KC, D])
        lnw_s = sb("lnw_s", [P, KC])
        lnb_s = sb("lnb_s", [P, KC])
        rw_s = sb("rw_s", [P, KC, RN])
        gu_s = sb("gu_s", [P, EXPERTS, KC, 2, 2, HALF])
        tok_s = sb("tok_s", [P, SEQS], I32)
        hash_s = sb("hash_s", [P, SEQS, 2], I32)
        new_base = sb("new_base", [P, D])
        base = sb("base", [P, 2, D])
        hidden = sb("hidden", [P, 2, D])
        place_of = sb("place_of", [P, EXPERTS], U32)
        choice = sb("choice", [P, SEQS, 2])

        region = sb("region", [P, EXPERTS * 6 * D])
        down_s = region[:, :].rearrange("p (e c n) -> p e c n", e=EXPERTS, c=6)
        used = [0]

        def part(*shape, dt=F32):
            n = 1
            for s in shape:
                n *= s
            words = n if dt != BF16 else n // 2
            a = region[:, used[0]:used[0] + words]
            used[0] += words
            assert used[0] <= EXPERTS * 6 * D
            if dt != F32:
                a = a.bitcast(dt)
            if len(shape) == 2:
                a = a.rearrange("p (a b) -> p a b", a=shape[0])
            if len(shape) == 3:
                a = a.rearrange("p (a b c) -> p a b c", a=shape[0], b=shape[1])
            return a

        pair_emb = part(2, 2 * RANK)
        emb_t = part(P)
        z = part(D)
        y_t = part(KC, P)
        q_masked = part(HEADS, P)
        k_t = part(2, KC, P)
        v_one = part(2, HEADS * VW + AVN)
        shifted = part(2, QH * P)
        probs = part(2, QH * P)
        probs_t = part(2, QH * P)
        attn = part(D)
        attn_t = part(KC, P)
        x2 = sb("x2", [P, 2, XW])
        logit = part(EXPERTS)
        sorted_l = part(EXPERTS)
        sorted_x = part(EXPERTS)
        exp_sum = part(1)
        exp_rec = part(1)
        x2_t = part(KC, P)
        rowmax = part(2, QH)
        recip = part(HEADS)
        bnF, mvF, aF, rF, nmF = part(6), part(2), part(2), part(2), part(2)
        bnO, mvO, aO, rO, nmO = part(6), part(2), part(2), part(2), part(2)
        gathered_idx = sb("gathered_idx", [P, 2, 2], I32)

        used[0] = DOWN_EARLY * 6 * D
        NE = SEQS * EXPERTS
        rmask_a, rmask_b, work_a = (part(SEQS, EXPERTS) for _ in range(3))
        cum_a, cum_b = part(SEQS, EXPERTS), part(SEQS, EXPERTS)
        both_h = part(SEQS, EXPERTS, dt=BF16)
        cum_h = part(SEQS + 1, EXPERTS, dt=BF16)
        count_f, count_i = part(EXPERTS), part(EXPERTS, dt=I32)
        tiles_i, tiles_f = part(EXPERTS, dt=I32), part(EXPERTS)
        ends, ends2, starts = part(EXPERTS), part(EXPERTS), part(EXPERTS)
        pos_f, pos_i = part(SEQS, 2), part(SEQS, 2, dt=I32)
        hi_i, lo_i = part(SEQS, 2, dt=I32), part(SEQS, 2, dt=I32)
        hi_f, lo_f = part(SEQS, 2), part(SEQS, 2)
        onehot_lo = part(2, GROUP * P, dt=BF16)
        onehot_hi = part(2, GROUP * 72)
        onehot_hv = part(2, 2 * GROUP * 72, dt=BF16)
        tab = part(2, TILES)
        pair_i, half_i = part(TILES, dt=I32), part(TILES, dt=I32)
        half_f, place_f, empty = part(TILES), part(TILES), part(TILES)
        cmp_f = part(TILES, EXPERTS)
        exp_f = part(TILES)
        second = sb("second", [P, TILES])
        first_c = sb("first_c", [P, TILES])
        slot_w = sb("slot_w", [P, TILES])
        w_part = sb("w_part", [P, 1])
        tok_of = sb("tok_of", [P, TILES], I32)
        row_of = sb("row_of", [P, TILES], I32)
        exp_of = sb("exp_of", [1, TILES], I32)

        tok_idx = sb("tok_idx", [P, 2], I32)
        row_idx = sb("row_idx", [P, 2], I32)
        xe = sb("xe", [P, 2, XW])
        xe_t = sb("xe_t", [P, 2, KC, P])
        silu = sb("silu", [P, 2, HALF])
        h_s = sb("h_s", [P, 2, HALF])
        h_t = sb("h_t", [P, 2, 3, P])
        y_s = sb("y_s", [P, 2, D])

        ld_tok, ld_att, ld_gu, ld_down = sem("ld_tok"), sem("ld_att"), sem("ld_gu"), sem("ld_down")
        const_v, const_p, const_q = sem("const_v"), sem("const_p"), sem("const_q")
        hashed = sem("hashed")
        idx_ready = sem("idx_ready")
        emb_in = [sem("emb_in0"), sem("emb_in1")]
        embT_ps, embT_sb, h_ps = sem("embT_ps"), sem("embT_sb"), sem("h_ps")
        f_bn, f_mv, f_a, f_pow, f_nm, f_r1, z_sb, sum_sb, base_sb = (
            sem(n) for n in ("f_bn", "f_mv", "f_a", "f_pow", "f_nm", "f_r1", "z_sb", "sum_sb", "base_sb"))
        zT_ps, yT_sb, qk_ps, k_sb, q_sb, v_ps, v_sb = (
            sem(n) for n in ("zT_ps", "yT_sb", "qk_ps", "k_sb", "q_sb", "v_ps", "v_sb"))
        s_ps, max_sb, shift_sb, exp_sb, pT_ps, pT_sb, av_ps = (
            sem(n) for n in ("s_ps", "max_sb", "shift_sb", "exp_sb", "pT_ps", "pT_sb", "av_ps"))
        rec_sb, attn_sb, attnT_ps, attnT_sb, o_ps, hid_sb = (
            sem(n) for n in ("rec_sb", "attn_sb", "attnT_ps", "attnT_sb", "o_ps", "hid_sb"))
        o_bn, o_mv, o_a, o_pow, o_nm, x2_sb = (
            sem(n) for n in ("o_bn", "o_mv", "o_a", "o_pow", "o_nm", "x2_sb"))
        x2_out = [sem("x2_out0"), sem("x2_out1")]
        x2T_ps, x2T_sb, lg_ps, lg_sb = sem("x2T_ps"), sem("x2T_sb"), sem("lg_ps"), sem("lg_sb")
        c_max, c_idx, c_put, c_sub, c_exp, c_rec, c_w = (
            sem(n) for n in ("c_max", "c_idx", "c_put", "c_sub", "c_exp", "c_rec", "c_w"))
        hid_out = [sem("hid_out0"), sem("hid_out1")]
        zero_sb, zero_out = sem("zero_sb"), sem("zero_out")
        route, rank_ps = sem("route"), sem("rank_ps")
        oh_lo, oh_hi, oh_hp, oh_hc, tab_mm = (
            sem(n) for n in ("oh_lo", "oh_hi", "oh_hp", "oh_hc", "tab_mm"))
        routed, counted = sem("routed"), sem("counted")
        tidx, ridx = sem("tidx"), sem("ridx")
        xe_in = [sem("xe_in0"), sem("xe_in1")]
        xeT_ps, xeT_sb = sem("xeT_ps"), sem("xeT_sb")
        gu_ps, silu_sb, hid2_sb, hT_ps, hT_sb, y_ps, y_sb = (
            sem(n) for n in ("gu_ps", "silu_sb", "hid2_sb", "hT_ps", "hT_sb", "y_ps", "y_sb"))
        w_half, w_slot = sem("w_half"), sem("w_slot")
        y_out = sem("y_out")

        block = ctx.enter_context(nc.Block())

        S = [bank[0], bank[1]]
        PT = [bank[2], bank[3]]
        AV, FB, VB, OB = bank[4], bank[5], bank[6], bank[7]
        N_ATT = 16 * 9
        N_EXP_CONST = 12

        def sequence(i):
            return At(i // 2, i % 2) if 0 <= i < SEQS else None

        def run_sequences(step, eng):
            for i in range(-2, 4):
                step(*(sequence(i + d) for d in (2, 1, 0, -1, -2)))
            with eng.Fori(2, SEQS // 2 - 1) as k:
                for u in range(2):
                    step(*(At(k, u).plus(d) for d in (2, 1, 0, -1, -2)))
            for i in range(SEQS - 2, SEQS + 2):
                step(*(sequence(i + d) for d in (2, 1, 0, -1, -2)))

        def tile_at(t):
            return At(t // 2, t % 2) if 0 <= t < TILES else None

        def run_tiles(step, eng):
            for t in range(4):
                step(*(tile_at(t + d) for d in (-1, 0, 1, 2)))
            with eng.Fori(2, (TILES - 3) // 2) as k:
                for u in range(2):
                    step(*(At(k, u).plus(d) for d in (-1, 0, 1, 2)))
            for t in range(2 * ((TILES - 3) // 2), TILES + 1):
                step(*(tile_at(t + d) for d in (-1, 0, 1, 2)))

        @block.sync
        def _(eng):
            eng.dma_start(tok_s[:, :], tokens).then_inc(ld_tok, 16)
            eng.dma_start(proj_s[0:RANK, :], proj).then_inc(ld_att, 16)
            eng.dma_start(proj_s[RANK:P, :], proj).then_inc(ld_att, 16)
            eng.dma_start(lnw_s[:, :], ln_w).then_inc(ld_att, 16)
            eng.dma_start(lnb_s[:, :], ln_b).then_inc(ld_att, 16)
            eng.dma_start(wqk_s[:, :, 0:D], wq).then_inc(ld_att, 16)
            eng.dma_start(wqk_s[:, :, D:2 * D], wk).then_inc(ld_att, 16)
            eng.dma_start(wv_s[:, :, :], wv).then_inc(ld_att, 16)
            eng.dma_start(wo_s[:, :, :], wo).then_inc(ld_att, 16)
            eng.dma_start(rw_s[:, :, :], router).then_inc(ld_att, 16)
            for e in range(EXPERTS):
                eng.dma_start(gu_s[:, e], gate_up[:, e]).then_inc(ld_gu, 16)

            eng.wait_ge(zero_sb, 1)
            eng.dma_start(out[TOKENS:TOKENS + P, :], y_s[:, 0, :]).then_inc(zero_out, 16)

            def store(at):
                eng.wait_ge(hid_sb, at.i + 1)
                eng.dma_start(out[bass.ds(at.i * SEQ, SEQ), :], hidden[:, at.u, :]).then_inc(hid_out[at.u], 16)
                eng.wait_ge(x2_sb, at.i + 1)
                eng.wait_ge(c_w, at.i + 1)
                eng.dma_start(xs[bass.ds(at.i * SEQ, SEQ), :], x2[:, at.u, :]).then_inc(x2_out[at.u], 16)

            with eng.Fori(0, SEQS // 2) as k:
                store(At(k, 0))
                store(At(k, 1))

            eng.wait_ge(lg_ps, SEQS)
            eng.wait_ge(counted, 1)
            for e in range(EXPERTS):
                if e == DOWN_EARLY:
                    eng.wait_ge(routed, 5)
                eng.dma_start(down_s[:, e], down[:, e]).then_inc(ld_down, 16)

            eng.wait_ge(y_out, 16 * TILES)

        @block.gpsimd
        def _(eng):
            eng.memset(ident[:, :], 0.0).then_inc(const_p, 1)
            eng.memset(headmask[:, :], 1.0).then_inc(const_p, 1)
            eng.memset(causal[:, :], 0.0).then_inc(const_p, 1)
            eng.memset(before[:, :], 1.0).then_inc(const_p, 1)
            eng.memset(minus_half[:, :], -0.5).then_inc(const_p, 1)
            eng.iota(row_of[:, :], pattern=[[1, TILES]], base=0, channel_multiplier=0).then_inc(const_p, 1)
            eng.iota(region[:, 0:P].bitcast(I32), pattern=[[1, P]], base=0, channel_multiplier=0).then_inc(const_p, 1)
            eng.iota(region[:, P:P + 1].bitcast(I32), pattern=[[1, 1]], base=1, channel_multiplier=1).then_inc(const_p, 1)
            eng.iota(region[:, 2 * P:2 * P + EXPERTS].bitcast(I32), pattern=[[1, EXPERTS]], base=0, channel_multiplier=0).then_inc(const_p, 1)
            eng.wait_ge(const_p, 9)
            eng.affine_select(out=ident[:, :], in_=ident[:, :], compare_op=ALU.not_equal, fill=1.0, base=0,
                              pattern=[[-1, P]], channel_multiplier=1).then_inc(const_q, 1)
            eng.affine_select(out=causal[:, :], in_=causal[:, :], compare_op=ALU.is_ge, fill=NEG, base=0,
                              pattern=[[0, QH], [-1, P]], channel_multiplier=1).then_inc(const_q, 1)
            eng.affine_select(out=before[:, :], in_=before[:, :], compare_op=ALU.is_gt, fill=0.0, base=0,
                              pattern=[[1, P]], channel_multiplier=-1).then_inc(const_q, 1)
            eng.affine_select(out=headmask[:, :], in_=headmask[:, :], compare_op=ALU.is_ge, fill=0.0, base=0,
                              pattern=[[-HD, 8]], channel_multiplier=1).then_inc(const_q, 1)
            eng.wait_ge(const_q, 4)
            eng.affine_select(out=headmask[:, :], in_=headmask[:, :], compare_op=ALU.is_ge, fill=0.0, base=HD - 1,
                              pattern=[[HD, 8]], channel_multiplier=-1).then_inc(const_q, 1)
            eng.wait_ge(hashed, 5)

            def gather(at):
                wait(eng, embT_ps, at.i - 1)
                eng.tensor_copy(gathered_idx[:, at.u, :], hash_s[:, at.i, :]).then_inc(idx_ready, 1)
                wait_apart(eng, idx_ready, at.i + 1, (hashed, 5))
                for c in range(2):
                    eng.indirect_dma_start(
                        out=pair_emb[:, at.u, c * RANK:(c + 1) * RANK], out_offset=None, in_=emb,
                        in_offset=bass.IndirectOffsetOnAxis(ap=gathered_idx[:, at.u, c:c + 1], axis=0),
                    ).then_inc(emb_in[at.u], 16)

            def step(early, front, mid, back, chosen):
                if front is not None:
                    eng.wait_ge(f_a, front.i + 1)
                    eng.tensor_tensor(rF[:, :], aF[:, :], minus_half[:, :], ALU.pow).then_inc(f_pow, 1)
                if early is not None:
                    gather(early)
                if back is not None:
                    eng.wait_ge(o_a, back.i + 1)
                    eng.tensor_tensor(rO[:, 0:1], aO[:, 0:1], minus_half[:, 0:1], ALU.pow).then_inc(o_pow, 1)
                if front is not None:
                    wait_apart(eng, sum_sb, front.i + 1, (hashed, 5))
                    wait(eng, hid_sb, front.i - 1)
                    eng.tensor_copy(base[:, front.u, :], new_base[:, :]).then_inc(base_sb, 1)

            run_sequences(step, eng)

            def weigh(g, u):
                wait_apart(eng, oh_hi, g + 1, (hashed, 5))
                if not isinstance(g, int):
                    wait_apart(eng, tab_mm, g - 1, (hashed, 5))
                hi = onehot_hi[:, u, 0:GROUP * TILES].rearrange("p (c t) -> p c t", c=GROUP)
                hv = onehot_hv[:, u, 0:2 * GROUP * TILES].rearrange("p (c v t) -> p c v t", c=GROUP, v=2)
                eng.tensor_tensor(hv[:, :, 1, :], hi,
                                  iota_pair[:, bass.ds(g * GROUP, GROUP)].unsqueeze(2).to_broadcast([P, GROUP, TILES]),
                                  ALU.mult).then_inc(oh_hc, 1)

            weigh(0, 0)
            weigh(1, 1)
            with eng.Fori(1, PAIRS // GROUP // 2) as k:
                weigh(2 * k, 0)
                weigh(2 * k + 1, 1)

            eng.wait_ge(routed, 5)
            for u in range(2):
                eng.wait_ge(x2_out[u], 16 * (SEQS // 2))
                eng.wait_ge(hid_out[u], 16 * (SEQS // 2))
            eng.wait_ge(zero_out, 16)

            def fetch(at):
                wait(eng, xeT_ps, at.i - 1)
                wait(eng, w_slot, at.i - 1)
                eng.tensor_copy(tok_idx[:, at.u:at.u + 1], tok_of[:, bass.ds(at.i, 1)]).then_inc(tidx, 1)
                wait_apart(eng, tidx, at.i + 1, (routed, 3))
                eng.indirect_dma_start(
                    out=xe[:, at.u, :], out_offset=None, in_=xs,
                    in_offset=bass.IndirectOffsetOnAxis(ap=tok_idx[:, at.u:at.u + 1], axis=0),
                ).then_inc(xe_in[at.u], 16)

            def scatter(at):
                wait(eng, y_out, 16 * at.i)
                eng.tensor_copy(row_idx[:, at.u:at.u + 1], row_of[:, bass.ds(at.i, 1)]).then_inc(ridx, 1)
                wait_apart(eng, ridx, at.i + 1, (routed, 3))
                eng.wait_ge(y_sb, at.i + 1)
                eng.indirect_dma_start(
                    out=out, out_offset=bass.IndirectOffsetOnAxis(ap=row_idx[:, at.u:at.u + 1], axis=0),
                    in_=y_s[:, at.u, :], in_offset=None, compute_op=ALU.add,
                ).then_inc(y_out, 16)

            fetch(At(0, 0))
            fetch(At(0, 1))

            def step(prev, at, nxt, after):
                if prev is not None:
                    scatter(prev)
                if at is not None and after is not None:
                    fetch(after)

            run_tiles(step, eng)

        @block.tensor
        def _(eng):
            eng.wait_ge(const_q, 5)
            eng.wait_ge(const_v, N_EXP_CONST)
            eng.wait_ge(ld_att, N_ATT)

            def scores(at, q):
                n = 4 * at.i + q
                if q == 0:
                    eng.wait_ge(k_sb, at.i + 1)
                eng.wait_ge(q_sb, n + 1)
                wait(eng, shift_sb, n - 1)
                s = S[q % 2]
                eng.matmul(s[:, :], identb[:, :], causal[:, :], start=True, stop=False)
                for h in range(QH):
                    mm = eng.matmul(s[:, h * P:(h + 1) * P], q_masked[:, q * QH + h, :], k_t[:, at.u, q // 2, :],
                                    start=False, stop=(h == QH - 1))
                mm.then_inc(s_ps, 1)

            def probs_turn(at, q):
                n = 4 * at.i + q
                eng.wait_ge(exp_sb, n + 1)
                wait(eng, pT_sb, n - 1)
                for h in range(QH):
                    mm = eng.transpose(PT[q % 2][:, h * P:(h + 1) * P], probs[:, q % 2, h * P:(h + 1) * P], ident[:, :])
                mm.then_inc(pT_ps, 1)

            def weigh_values(at, q):
                n = 4 * at.i + q
                eng.wait_ge(pT_sb, n + 1)
                if q == 0:
                    eng.wait_ge(v_sb, at.i + 1)
                    wait(eng, attn_sb, at.i)
                for h in range(QH):
                    c = (q * QH + h) * VW
                    mm = eng.matmul(AV[:, c:c + AVN], probs_t[:, q % 2, h * P:(h + 1) * P], v_one[:, at.u, c:c + AVN],
                                    start=True, stop=True)
                mm.then_inc(av_ps, 1)

            def turn(dst, src, done):
                for c in range(KC):
                    mm = eng.transpose(dst[:, c * P:(c + 1) * P], src[:, c * P:(c + 1) * P], ident[:, :])
                mm.then_inc(done, 1)

            def step(early, front, mid, back, chosen):
                if mid is not None:
                    probs_turn(mid, 0)
                    scores(mid, 2)
                if back is not None:
                    eng.wait_ge(attn_sb, back.i + 1)
                    wait(eng, lg_sb, back.i)
                    turn(OB, attn, attnT_ps)
                if mid is not None:
                    probs_turn(mid, 1)
                    weigh_values(mid, 0)
                if front is not None:
                    eng.wait_ge(z_sb, front.i + 1)
                    eng.wait_ge(sum_sb, front.i + 1)
                    turn(FB, z, zT_ps)
                if back is not None:
                    eng.wait_ge(attnT_sb, back.i + 1)
                    for c in range(KC):
                        mm = eng.matmul(OB[:, D:2 * D], attn_t[:, c, :], wo_s[:, c, :], start=(c == 0), stop=(c == KC - 1))
                    mm.then_inc(o_ps, 1)
                if mid is not None:
                    scores(mid, 3)
                if front is not None:
                    eng.wait_ge(yT_sb, front.i + 1)
                    for m in range(4):
                        for c in range(KC):
                            mm = eng.matmul(FB[:, m * P:(m + 1) * P], wqk_s[:, c, m * P:(m + 1) * P], y_t[:, c, :],
                                            start=(c == 0), stop=(c == KC - 1))
                    mm.then_inc(qk_ps, 1)
                if mid is not None:
                    probs_turn(mid, 2)
                    weigh_values(mid, 1)
                if front is not None:
                    wait(eng, v_sb, front.i)
                    for c in range(KC):
                        mm = eng.matmul(VB[:, 0:D], y_t[:, c, :], wv_s[:, c, :], start=(c == 0), stop=(c == KC - 1))
                    mm.then_inc(v_ps, 1)
                if mid is not None:
                    weigh_values(mid, 2)
                if front is not None:
                    scores(front, 0)
                if back is not None:
                    eng.wait_ge(x2_sb, back.i + 1)
                    turn(OB, x2[:, back.u, 0:D], x2T_ps)
                if mid is not None:
                    probs_turn(mid, 3)
                if early is not None:
                    eng.wait_ge(emb_in[early.u], 32 * (early.k + 1))
                    wait(eng, q_sb, 4 * early.i)
                    wait(eng, k_sb, early.i)
                    eng.transpose(FB[:, 0:P], pair_emb[:, early.u, :], ident[:, :]).then_inc(embT_ps, 1)
                if front is not None:
                    scores(front, 1)
                if back is not None:
                    eng.wait_ge(x2T_sb, back.i + 1)
                    for c in range(KC):
                        mm = eng.matmul(OB[:, D:D + RN], x2_t[:, c, :], rw_s[:, c, :], start=(c == 0), stop=(c == KC - 1))
                    mm.then_inc(lg_ps, 1)
                if mid is not None:
                    weigh_values(mid, 3)
                if early is not None:
                    eng.wait_ge(embT_sb, early.i + 1)
                    eng.matmul(FB[:, P:P + D], emb_t[:, :], proj_s[:, :], start=True, stop=True).then_inc(h_ps, 1)

            run_sequences(step, eng)

            eng.wait_ge(counted, 1)
            bh = both_h.rearrange("p a b -> p (a b)")
            eng.matmul(bank[0][:, 0:NE], before[:, :], bh, start=True, stop=False)
            eng.matmul(bank[0][:, 0:NE], onesb[:, :], cum_h[:, 0:SEQS, :].rearrange("p a b -> p (a b)"), start=False, stop=True).then_inc(rank_ps, 1)
            eng.matmul(bank[1][:, 0:EXPERTS], onesb[:, :], cum_h[:, SEQS, :], start=True, stop=True).then_inc(rank_ps, 1)

            def fill(g, u, first=False, last=False):
                eng.wait_ge(oh_lo, g + 1)
                eng.wait_ge(oh_hp, g + 1)
                eng.wait_ge(oh_hc, g + 1)
                for c in range(GROUP):
                    mm = eng.matmul(bank[2][:, 0:2 * TILES], onehot_lo[:, u, c * P:(c + 1) * P],
                                    onehot_hv[:, u, c * 2 * TILES:(c + 1) * 2 * TILES],
                                    start=(first and c == 0), stop=(last and c == GROUP - 1))
                mm.then_inc(tab_mm, 1)

            groups = PAIRS // GROUP
            fill(0, 0, first=True)
            fill(1, 1)
            with eng.Fori(1, groups // 2 - 1) as k:
                fill(2 * k, 0)
                fill(2 * k + 1, 1)
            fill(groups - 2, 0)
            fill(groups - 1, 1, last=True)

            eng.wait_ge(routed, 5)
            eng.wait_ge(ld_gu, 16 * EXPERTS)

            def tokens_turn(at):
                eng.wait_ge(xe_in[at.u], 16 * (at.k + 1))
                wait(eng, xeT_sb, at.i)
                turn(bank[7], xe[:, at.u, :], xeT_ps)

            def widen(at, e, half):
                if half == 0:
                    eng.wait_ge(xeT_sb, at.i + 1)
                wait(eng, hid2_sb, 2 * at.i + half - 1)
                for g in range(2):
                    for c in range(KC):
                        mm = eng.matmul(bank[2 * half + g][:, 0:HALF], xe_t[:, at.u, c, :], gu_s[:, e, c, half, g, :],
                                        start=(c == 0), stop=(c == KC - 1))
                mm.then_inc(gu_ps, 1)

            def inner_turn(at, half):
                n = 2 * at.i + half
                eng.wait_ge(hid2_sb, n + 1)
                wait(eng, hT_sb, n - 1)
                for c, w in enumerate(CHUNKS):
                    mm = eng.transpose(bank[4 + half][0:w, c * P:(c + 1) * P], h_s[:, half, c * P:c * P + w], ident[:, :])
                mm.then_inc(hT_ps, 1)

            def narrow(at, e):
                eng.wait_ge(hT_sb, 2 * at.i + 2)
                wait(eng, y_sb, at.i)
                for half in range(2):
                    for c, w in enumerate(CHUNKS):
                        mm = eng.matmul(bank[6][:, 0:D], h_t[0:w, half, c, :], down_s[0:w, e, 3 * half + c, :],
                                        start=(half == 0 and c == 0), stop=(half == 1 and c == 2))
                mm.then_inc(y_ps, 1)

            def expert_of(at):
                return eng.value_load(exp_of[0:1, bass.ds(at.i, 1)], min_val=0, max_val=EXPERTS - 1)

            tokens_turn(tile_at(0))

            def step(prev, at, nxt, after):
                if at is not None:
                    e = expert_of(at)
                    widen(at, e, 0)
                    widen(at, e, 1)
                if prev is not None:
                    if isinstance(prev.i, int) and prev.i == 0:
                        eng.wait_ge(ld_down, 16 * EXPERTS)
                    narrow(prev, expert_of(prev))
                if nxt is not None:
                    tokens_turn(nxt)
                if at is not None:
                    inner_turn(at, 0)
                    inner_turn(at, 1)

            run_tiles(step, eng)

        @block.scalar
        def _(eng):
            eng.wait_ge(ld_att, N_ATT)

            def exps(at, q):
                n = 4 * at.i + q
                eng.wait_ge(shift_sb, n + 1)
                wait(eng, pT_ps, n - 1)
                eng.activation(probs[:, q % 2, :], shifted[:, q % 2, :], ACT.Exp, scale=SCALE).then_inc(exp_sb, 1)

            def probs_copy(at, q):
                n = 4 * at.i + q
                eng.wait_ge(pT_ps, n + 1)
                wait(eng, av_ps, n - 1)
                eng.copy(probs_t[:, q % 2, :], PT[q % 2][:, :]).then_inc(pT_sb, 1)

            def step(early, front, mid, back, chosen):
                if mid is not None:
                    probs_copy(mid, 0)
                if chosen is not None:
                    eng.wait_ge(c_sub, chosen.i + 1)
                    eng.activation(sorted_x, sorted_x, ACT.Exp, accum_out=exp_sum).then_inc(c_exp, 1)
                if back is not None:
                    eng.wait_ge(attnT_ps, back.i + 1)
                    wait(eng, o_ps, back.i)
                    eng.copy(attn_t.rearrange("p a b -> p (a b)"), OB[:, 0:D]).then_inc(attnT_sb, 1)
                if mid is not None:
                    probs_copy(mid, 1)
                if front is not None:
                    eng.wait_ge(zT_ps, front.i + 1)
                    wait(eng, v_ps, front.i)
                    for c in range(KC):
                        act = eng.activation(y_t[:, c, :], FB[:, c * P:(c + 1) * P], ACT.Identity,
                                             bias=lnb_s[:, c:c + 1], scale=lnw_s[:, c:c + 1])
                    act.then_inc(yT_sb, 1)
                if mid is not None:
                    exps(mid, 2)
                if front is not None:
                    eng.wait_ge(qk_ps, front.i + 1)
                    wait(eng, s_ps, 4 * front.i - 4)
                    eng.copy(k_t[:, front.u].rearrange("p a b -> p (a b)"), FB[:, 2 * P:4 * P]).then_inc(k_sb, 1)
                if mid is not None:
                    exps(mid, 3)
                    probs_copy(mid, 2)
                if front is not None:
                    eng.wait_ge(v_ps, front.i + 1)
                    wait(eng, av_ps, 4 * front.i - 4)
                    eng.copy(v_one[:, front.u, 0:HEADS * VW].rearrange("p (h v) -> p h v", v=VW)[:, :, 0:HD],
                             VB[:, 0:D].rearrange("p (h v) -> p h v", v=HD)).then_inc(v_sb, 1)
                if back is not None:
                    eng.wait_ge(x2T_ps, back.i + 1)
                    wait(eng, lg_ps, back.i)
                    eng.copy(x2_t.rearrange("p a b -> p (a b)"), OB[:, 0:D]).then_inc(x2T_sb, 1)
                if mid is not None:
                    probs_copy(mid, 3)
                if early is not None:
                    eng.wait_ge(embT_ps, early.i + 1)
                    wait(eng, h_ps, early.i)
                    eng.mul(emb_t[:, :], FB[:, 0:P], 0.5).then_inc(embT_sb, 1)
                if front is not None:
                    exps(front, 0)
                    exps(front, 1)

            run_sequences(step, eng)

            def weigh(g, u):
                eng.wait_ge(oh_hi, g + 1)
                wait(eng, tab_mm, g - 1)
                hi = onehot_hi[:, u, 0:GROUP * TILES].rearrange("p (c t) -> p c t", c=GROUP)
                hv = onehot_hv[:, u, 0:2 * GROUP * TILES].rearrange("p (c v t) -> p c v t", c=GROUP, v=2)
                eng.activation(hv[:, :, 0, :], hi, ACT.Identity, scale=place1[:, 0:1]).then_inc(oh_hp, 1)

            weigh(0, 0)
            weigh(1, 1)
            with eng.Fori(1, PAIRS // GROUP // 2) as k:
                weigh(2 * k, 0)
                weigh(2 * k + 1, 1)

            def turned(at):
                eng.wait_ge(xeT_ps, at.i + 1)
                wait(eng, gu_ps, 2 * at.i - 2)
                eng.copy(xe_t[:, at.u].rearrange("p a b -> p (a b)"), bank[7][:, 0:D]).then_inc(xeT_sb, 1)

            turned(tile_at(0))

            def step(prev, at, nxt, after):
                if at is None:
                    return
                for half in range(2):
                    n = 2 * at.i + half
                    eng.wait_ge(gu_ps, n + 1)
                    wait(eng, hid2_sb, n - 1)
                    eng.activation(silu[:, half, :], bank[2 * half][:, 0:HALF], ACT.Silu).then_inc(silu_sb, 1)
                if nxt is not None:
                    turned(nxt)
                for half in range(2):
                    n = 2 * at.i + half
                    eng.wait_ge(hT_ps, n + 1)
                    wait(eng, y_ps, at.i)
                    eng.copy(h_t[:, half, 0:2].rearrange("p a b -> p (a b)"), bank[4 + half][:, 0:2 * P])
                    eng.copy(h_t[0:CHUNKS[2], half, 2], bank[4 + half][0:CHUNKS[2], 2 * P:3 * P]).then_inc(hT_sb, 1)

            run_tiles(step, eng)

        @block.vector
        def _(eng):
            eng.memset(y_s[:, 0, :], 0.0).then_inc(zero_sb, 1)
            eng.memset(onesb[:, :], 1.0).then_inc(const_v, 1)
            eng.memset(ln_mul[:, 0:1], 1.0).then_inc(const_v, 1)
            eng.memset(ln_mul[:, 1:2], 1.0 + EPS).then_inc(const_v, 1)
            eng.memset(ln_add[:, 0:1], EPS).then_inc(const_v, 1)
            eng.memset(ln_add[:, 1:2], EPS * EPS).then_inc(const_v, 1)
            eng.wait_ge(const_p, 9)
            eng.tensor_scalar(trash_row[:, :], region[:, P:P + 1].bitcast(I32), float(TOKENS - 1), None,
                              ALU.add).then_inc(const_v, 1)
            eng.tensor_copy(iota_tile[:, :], row_of[:, :]).then_inc(const_v, 1)
            eng.tensor_copy(iota_lo[:, :], region[:, 0:P].bitcast(I32)).then_inc(const_v, 1)
            eng.tensor_copy(place1[:, :], region[:, P:P + 1].bitcast(I32)).then_inc(const_v, 1)
            eng.tensor_copy(iota_expert[:, :], region[:, 2 * P:2 * P + EXPERTS].bitcast(I32)).then_inc(const_v, 1)
            eng.wait_ge(const_q, 1)
            eng.tensor_copy(identb[:, :], ident[:, :]).then_inc(const_v, 1)
            eng.wait_ge(const_v, 11)
            eng.tensor_copy(iota_pair[:, :], iota_lo[:, 0:PAIRS])
            eng.memset(v_one.rearrange("p a b -> p (a b)"), 1.0).then_inc(const_v, 1)

            eng.wait_ge(ld_tok, 16)
            eng.tensor_scalar(tok_s[:, :], tok_s[:, :], BUCKETS - 1, None, ALU.bitwise_and).then_inc(hashed, 1)
            eng.wait_ge(hashed, 1)
            eng.tensor_scalar(hash_s[:, :, 0], tok_s[:, :], 31.0, 7.0, ALU.mult, ALU.add).then_inc(hashed, 1)
            eng.tensor_scalar(hash_s[:, :, 1], tok_s[:, :], 131.0, 13.0, ALU.mult, ALU.add).then_inc(hashed, 1)
            eng.wait_ge(hashed, 3)
            for c in range(2):
                eng.tensor_scalar(hash_s[:, :, c], hash_s[:, :, c], BUCKETS - 1, None, ALU.bitwise_and).then_inc(hashed, 1)

            def softmax_shift(at, q):
                n = 4 * at.i + q
                s = S[q % 2][:, :].rearrange("p (h t) -> p h t", h=QH)
                eng.wait_ge(s_ps, n + 1)
                eng.tensor_reduce(rowmax[:, q % 2, :], s, AX, ALU.max).then_inc(max_sb, 1)
                eng.wait_ge(max_sb, n + 1)
                wait(eng, exp_sb, n - 1)
                eng.tensor_tensor(shifted[:, q % 2, :].rearrange("p (h t) -> p h t", h=QH), s,
                                  rowmax[:, q % 2, :].unsqueeze(2).to_broadcast([P, QH, P]), ALU.subtract).then_inc(shift_sb, 1)

            def queries(front, q):
                if q == 0:
                    eng.wait_ge(k_sb, front.i + 1)
                wait(eng, s_ps, 4 * front.i + q - 3)
                g = q // 2
                eng.tensor_tensor(q_masked[:, q * QH:(q + 1) * QH, :],
                                  FB[:, g * P:(g + 1) * P].unsqueeze(1).to_broadcast([P, QH, P]),
                                  headmask[:, (q % 2) * QH:(q % 2 + 1) * QH].unsqueeze(2).to_broadcast([P, QH, P]),
                                  ALU.mult).then_inc(q_sb, 1)

            def step(early, front, mid, back, chosen):
                if back is not None:
                    eng.wait_ge(av_ps, 4 * back.i + 4)
                    o = AV[:, 0:HEADS * VW].rearrange("p (h v) -> p h v", v=VW)
                    eng.reciprocal(recip[:, :], o[:, :, HD]).then_inc(rec_sb, 1)
                if chosen is not None:
                    wait_apart(eng, lg_sb, chosen.i + 1, (hashed, 5))
                    eng.max(sorted_l, logit).then_inc(c_max, 1)
                if back is not None:
                    eng.wait_ge(rec_sb, back.i + 1)
                    wait(eng, attnT_ps, back.i)
                    eng.tensor_tensor(attn.rearrange("p (h v) -> p h v", v=HD), o[:, :, 0:HD],
                                      recip.unsqueeze(2).to_broadcast([P, HEADS, HD]), ALU.mult).then_inc(attn_sb, 1)
                if front is not None:
                    wait_apart(eng, h_ps, front.i + 1, (hashed, 5))
                    h = FB[:, P:P + D]
                    eng.bn_stats(bnF[:, :], h).then_inc(f_bn, 1)
                if chosen is not None:
                    eng.wait_ge(c_max, chosen.i + 1)
                    eng.tensor_scalar(sorted_x, sorted_l, sorted_l[:, 0:1], None, ALU.subtract).then_inc(c_sub, 1)
                if front is not None:
                    wait_apart(eng, f_bn, front.i + 1, (hashed, 5))
                    eng.bn_aggr(mvF[:, :], bnF[:, :]).then_inc(f_mv, 1)
                if chosen is not None:
                    eng.max_index(place_of[:, :], sorted_l, logit).then_inc(c_idx, 1)
                if front is not None:
                    eng.wait_ge(f_mv, front.i + 1)
                    eng.scalar_tensor_tensor(out=aF[:, :], in0=ln_mul[:, :], scalar=mvF[:, 1:2], in1=ln_add[:, :],
                                             op0=ALU.mult, op1=ALU.add).then_inc(f_a, 1)
                if chosen is not None:
                    eng.wait_ge(c_idx, chosen.i + 1)
                    eng.tensor_copy(choice[:, chosen.i, :], place_of[:, 0:2]).then_inc(c_put, 1)
                    eng.wait_ge(c_exp, chosen.i + 1)
                    eng.reciprocal(exp_rec, exp_sum).then_inc(c_rec, 1)
                if front is not None:
                    eng.wait_ge(f_pow, front.i + 1)
                    eng.tensor_scalar(nmF[:, :], rF[:, :], mvF[:, 0:1], -1.0, ALU.mult, ALU.mult).then_inc(f_nm, 1)
                    eng.tensor_scalar(aF[:, 0:1], rF[:, 0:1], 1.0, None, ALU.add).then_inc(f_r1, 1)
                if chosen is not None:
                    eng.wait_ge(c_rec, chosen.i + 1)
                    eng.tensor_scalar(x2[:, chosen.u, D:D + 2], sorted_x[:, 0:2], exp_rec, None, ALU.mult).then_inc(c_w, 1)
                if front is not None:
                    eng.wait_ge(f_nm, front.i + 1)
                    wait(eng, zT_ps, front.i)
                    eng.tensor_scalar(z[:, :], h, rF[:, 1:2], nmF[:, 1:2], ALU.mult, ALU.add).then_inc(z_sb, 1)
                    eng.wait_ge(f_r1, front.i + 1)
                    wait(eng, base_sb, front.i)
                    eng.tensor_scalar(new_base[:, :], h, aF[:, 0:1], nmF[:, 0:1], ALU.mult, ALU.add).then_inc(sum_sb, 1)
                if mid is not None:
                    softmax_shift(mid, 2)
                if back is not None:
                    eng.wait_ge(base_sb, back.i + 1)
                    eng.wait_ge(o_ps, back.i + 1)
                    wait(eng, hid_out[back.u], 16 * back.k)
                    eng.tensor_tensor(hidden[:, back.u, :], OB[:, D:2 * D], base[:, back.u, :], ALU.add).then_inc(hid_sb, 1)
                    wait_apart(eng, hid_sb, back.i + 1, (hashed, 5))
                    eng.bn_stats(bnO[:, :], hidden[:, back.u, :]).then_inc(o_bn, 1)
                    wait_apart(eng, o_bn, back.i + 1, (hashed, 5))
                    eng.bn_aggr(mvO[:, :], bnO[:, :]).then_inc(o_mv, 1)
                    eng.wait_ge(o_mv, back.i + 1)
                    eng.tensor_scalar(aO[:, 0:1], mvO[:, 1:2], EPS, None, ALU.add).then_inc(o_a, 1)
                if mid is not None:
                    softmax_shift(mid, 3)
                if back is not None:
                    eng.wait_ge(o_pow, back.i + 1)
                    eng.tensor_scalar(nmO[:, 0:1], rO[:, 0:1], mvO[:, 0:1], -1.0, ALU.mult, ALU.mult).then_inc(o_nm, 1)
                if front is not None:
                    queries(front, 0)
                if back is not None:
                    eng.wait_ge(o_nm, back.i + 1)
                    wait(eng, x2T_ps, back.i - 1)
                    wait(eng, x2_out[back.u], 16 * back.k)
                    eng.tensor_scalar(x2[:, back.u, 0:D], hidden[:, back.u, :], rO[:, 0:1], nmO[:, 0:1], ALU.mult,
                                      ALU.add).then_inc(x2_sb, 1)
                if front is not None:
                    for q in range(1, QUARTERS):
                        queries(front, q)
                    softmax_shift(front, 0)
                    softmax_shift(front, 1)
                if back is not None:
                    eng.wait_ge(lg_ps, back.i + 1)
                    eng.tensor_copy(logit, OB[:, D:D + EXPERTS]).then_inc(lg_sb, 1)

            run_sequences(step, eng)

            steps = [0]

            def done(instruction):
                steps[0] += 1
                instruction.then_inc(route, 1)
                eng.wait_ge(route, steps[0])

            eng.wait_ge(c_put, SEQS)
            numbers = iota_expert[:, :].unsqueeze(1).to_broadcast([P, SEQS, EXPERTS])
            for c, m in enumerate((rmask_a, rmask_b)):
                done(eng.tensor_tensor(m, numbers, choice[:, :, c].unsqueeze(2).to_broadcast([P, SEQS, EXPERTS]),
                                       ALU.is_equal))
            done(eng.tensor_tensor(cum_a, rmask_a, rmask_b, ALU.add))
            src, dst, shift = cum_a, cum_b, 1
            while shift < SEQS:
                steps[0] += 2
                eng.tensor_copy(dst[:, 0:shift, :], src[:, 0:shift, :]).then_inc(route, 1)
                eng.tensor_tensor(dst[:, shift:, :], src[:, shift:, :], src[:, 0:SEQS - shift, :], ALU.add).then_inc(route, 1)
                eng.wait_ge(route, steps[0])
                src, dst, shift = dst, src, 2 * shift
            done(eng.memset(cum_h[:, 0, :], 0.0))
            done(eng.tensor_copy(cum_h[:, 1:, :], src))
            eng.tensor_tensor(both_h, rmask_a, rmask_b, ALU.add).then_inc(counted, 1)
            eng.wait_ge(rank_ps, 2)
            done(eng.tensor_scalar(count_i, bank[1][:, 0:EXPERTS], float(P - 1), None, ALU.add))
            done(eng.tensor_scalar(tiles_i, count_i, 7, None, ALU.arith_shift_right))
            done(eng.tensor_copy(tiles_f, tiles_i))
            a, b, shift = tiles_f, ends, 1
            for shift, a, b in ((1, tiles_f, ends), (2, ends, ends2), (4, ends2, ends)):
                steps[0] += 2
                eng.tensor_copy(b[:, 0:shift], a[:, 0:shift]).then_inc(route, 1)
                eng.tensor_tensor(b[:, shift:], a[:, shift:], a[:, 0:EXPERTS - shift], ALU.add).then_inc(route, 1)
                eng.wait_ge(route, steps[0])
            done(eng.tensor_tensor(starts, ends, tiles_f, ALU.subtract))
            done(eng.tensor_scalar(starts, starts, float(P), None, ALU.mult))
            done(eng.tensor_tensor(work_a, bank[0][:, 0:NE].rearrange("p (a b) -> p a b", b=EXPERTS),
                                   starts.unsqueeze(1).to_broadcast([P, SEQS, EXPERTS]), ALU.add))
            for c, m in enumerate((rmask_a, rmask_b)):
                done(eng.tensor_tensor(cum_a, work_a, m, ALU.mult))
                done(eng.tensor_reduce(pos_f[:, :, c], cum_a, AX, ALU.add))
            done(eng.tensor_copy(pos_i, pos_f))
            done(eng.tensor_scalar(hi_i, pos_i, 7, None, ALU.arith_shift_right))
            done(eng.tensor_scalar(lo_i, pos_i, P - 1, None, ALU.bitwise_and))
            done(eng.tensor_copy(hi_f, hi_i))
            done(eng.tensor_copy(lo_f, lo_i))

            def onehots(g, u):
                wait(eng, tab_mm, g - 1)
                lo = lo_f.rearrange("p a b -> p (a b)")[:, bass.ds(g * GROUP, GROUP)]
                hi = hi_f.rearrange("p a b -> p (a b)")[:, bass.ds(g * GROUP, GROUP)]
                eng.tensor_tensor(onehot_lo[:, u, :].rearrange("p (c t) -> p c t", c=GROUP),
                                  iota_lo[:, :].unsqueeze(1).to_broadcast([P, GROUP, P]),
                                  lo.unsqueeze(2).to_broadcast([P, GROUP, P]), ALU.is_equal).then_inc(oh_lo, 1)
                wait(eng, oh_hc, g - 1)
                eng.tensor_tensor(onehot_hi[:, u, 0:GROUP * TILES].rearrange("p (c t) -> p c t", c=GROUP),
                                  iota_tile[:, :].unsqueeze(1).to_broadcast([P, GROUP, TILES]),
                                  hi.unsqueeze(2).to_broadcast([P, GROUP, TILES]), ALU.is_equal).then_inc(oh_hi, 1)

            onehots(0, 0)
            onehots(1, 1)
            with eng.Fori(1, PAIRS // GROUP // 2) as k:
                onehots(2 * k, 0)
                onehots(2 * k + 1, 1)

            done(eng.tensor_tensor(cmp_f, iota_tile[:, :].unsqueeze(2).to_broadcast([P, TILES, EXPERTS]),
                                   ends.unsqueeze(1).to_broadcast([P, TILES, EXPERTS]), ALU.is_ge))
            done(eng.tensor_reduce(exp_f, cmp_f, AX, ALU.add))
            eng.tensor_scalar(exp_of[:, :], exp_f[0:1, :], float(EXPERTS - 1), None, ALU.min).then_inc(routed, 1)
            eng.wait_ge(tab_mm, PAIRS // GROUP)
            done(eng.tensor_copy(tab.rearrange("p a b -> p (a b)"), bank[2][:, 0:2 * TILES]))
            place, pair = tab[:, 0, :], tab[:, 1, :]
            done(eng.tensor_copy(pair_i, pair))
            done(eng.tensor_scalar(half_i, pair_i, 1, None, ALU.arith_shift_right))
            done(eng.tensor_copy(half_f, half_i))
            done(eng.tensor_scalar(place_f, place, -1.0, 0.0, ALU.add, ALU.max))
            done(eng.scalar_tensor_tensor(out=place_f, in0=half_f, scalar=float(P), in1=place_f, op0=ALU.mult, op1=ALU.add))
            eng.tensor_copy(tok_of[:, :], place_f).then_inc(routed, 1)
            done(eng.tensor_scalar(empty, place, 0.0, trash_row[:, 0:1], ALU.is_equal, ALU.mult))
            eng.tensor_tensor(row_of[:, :], empty, place_f, ALU.add).then_inc(routed, 1)
            done(eng.scalar_tensor_tensor(out=second[:, :], in0=half_f, scalar=-2.0, in1=pair, op0=ALU.mult, op1=ALU.add))
            eng.tensor_scalar(first_c[:, :], second[:, :], -1.0, 1.0, ALU.mult, ALU.add).then_inc(routed, 1)
            eng.tensor_copy(exp_f, place_f).then_inc(routed, 1)
            eng.wait_ge(routed, 5)

            def product(at, half):
                n = 2 * at.i + half
                eng.wait_ge(silu_sb, n + 1)
                wait(eng, hT_ps, n - 1)
                eng.tensor_tensor(h_s[:, half, :], bank[2 * half + 1][:, 0:HALF], silu[:, half, :], ALU.mult).then_inc(hid2_sb, 1)

            def slot_weight(at):
                eng.wait_ge(xe_in[at.u], 16 * (at.k + 1))
                eng.tensor_tensor(w_part[:, :], xe[:, at.u, D:D + 1], first_c[:, bass.ds(at.i, 1)], ALU.mult).then_inc(w_half, 1)
                eng.wait_ge(w_half, at.i + 1)
                eng.scalar_tensor_tensor(out=slot_w[:, bass.ds(at.i, 1)], in0=xe[:, at.u, D + 1:D + 2],
                                         scalar=second[:, bass.ds(at.i, 1)], in1=w_part[:, :], op0=ALU.mult,
                                         op1=ALU.add).then_inc(w_slot, 1)

            def result(at):
                eng.wait_ge(y_ps, at.i + 1)
                wait(eng, y_out, 16 * (at.i - 1))
                eng.tensor_scalar(y_s[:, at.u, :], bank[6][:, 0:D], slot_w[:, bass.ds(at.i, 1)], None,
                                  ALU.mult).then_inc(y_sb, 1)

            eng.wait_ge(zero_out, 16)

            def step(prev, at, nxt, after):
                if at is not None:
                    product(at, 0)
                    slot_weight(at)
                    product(at, 1)
                if prev is not None:
                    result(prev)

            run_tiles(step, eng)


def kernel(x, L0_tok_weight, L0_tok_proj, L0_attn_ln_w, L0_attn_ln_b, L0_attn_wq, L0_attn_wk, L0_attn_wv,
           L0_attn_wo, L0_ffn_router_w, L0_ffn_gate_w, L0_ffn_up_w, L0_ffn_down_w):
    import numpy as np
    import concourse.bacc as bacc
    from concourse.bass_utils import run_bass_kernel_spmd

    def chunks(a):
        return np.asarray(a).reshape(KC, P, -1).transpose(1, 0, 2)

    def heads(a):
        return np.asarray(a).transpose(1, 0, 2).reshape(D, D)

    router = np.zeros((D, RN), np.float32)
    router[:, :EXPERTS] = np.asarray(L0_ffn_router_w).T
    gate, up = (np.asarray(w).reshape(EXPERTS, 2, HALF, KC, P).transpose(4, 0, 3, 1, 2)
                for w in (L0_ffn_gate_w, L0_ffn_up_w))
    gate_up = np.stack([gate, up], axis=4)
    by_inner = np.asarray(L0_ffn_down_w).transpose(0, 2, 1)
    down = np.zeros((P, EXPERTS, 6, D), np.float32)
    for half in range(2):
        for c, w in enumerate(CHUNKS):
            at = half * HALF + c * P
            down[:w, :, 3 * half + c] = by_inner[:, at:at + w].transpose(1, 0, 2)
    arrays = {
        "tokens": np.asarray(x).T, "emb": L0_tok_weight, "proj": L0_tok_proj,
        "ln_w": np.asarray(L0_attn_ln_w).reshape(KC, P).T, "ln_b": np.asarray(L0_attn_ln_b).reshape(KC, P).T,
        "wq": chunks(heads(L0_attn_wq)), "wk": chunks(heads(L0_attn_wk)), "wv": chunks(heads(L0_attn_wv)),
        "wo": chunks(L0_attn_wo), "router": chunks(router), "gate_up": gate_up, "down": down,
    }
    nc = bacc.Bacc("TRN2", target_bir_lowering=False, num_devices=1)
    ins, args = {}, []
    for name, a in arrays.items():
        ins["in_" + name] = np.ascontiguousarray(a)
        args.append(nc.dram_tensor("in_" + name, ins["in_" + name].shape,
                                   mybir.dt.from_np(ins["in_" + name].dtype), kind="ExternalInput").ap())
    out = nc.dram_tensor("out_hidden", (TOKENS + P, D), F32, kind="ExternalOutput").ap()
    build(nc, *args, out)
    return run_bass_kernel_spmd(nc, [ins], core_ids=[0]).results[0]["out_hidden"][:TOKENS].reshape(SEQS, SEQ, D)
```

```python
from contextlib import ExitStack

import concourse.bass as bass
from concourse import mybir

F32 = mybir.dt.float32
BF16 = mybir.dt.bfloat16
F16 = mybir.dt.float16
I32 = mybir.dt.int32
U32 = mybir.dt.uint32
ALU = mybir.AluOpType
ACT = mybir.ActivationFunctionType
AX = mybir.AxisListType.X

P = 128
SEQS, SEQ = 32, 128
BUCKETS, RANK = 16384, 64
D, KC = 256, 2
HEADS, HD = 16, 16
EXPERTS, INNER = 8, 704
HALF = INNER // 2
CHUNKS = (P, P, HALF - 2 * P)
EPS = 1e-5
NEG = -1e30
QUARTERS, QH = 4, 4
VW = HD + 1
TOP = 15
X_EXP = TOP - 4
X_SCALE = 2.0 ** X_EXP
BIAS = 127
LEAST = 67
ONE_EXPONENT = 2.0 ** 23
UNIT = 2 * HALF
DOWN_UNIT = len(CHUNKS) * D
FIRST_K = 4
AVN = 96
RN = 96
PAIRS = 2 * SEQS
TILES = (2 * SEQS * SEQ + EXPERTS * (P - 1)) // P
TOKENS = SEQS * SEQ
XW = D + 2
GROUP = 8
SCALE = HD ** -0.5


class At:

    def __init__(self, k, u):
        self.k, self.u = k, u
        self.i = 2 * k + u

    def plus(self, n):
        u = self.u + n
        return At(self.k + u // 2 if u // 2 else self.k, u % 2)


def wait(eng, sem, value):
    if isinstance(value, int) and value <= 0:
        return
    eng.wait_ge(sem, value)


def waits_apart(eng, met, *waits):
    waits = [(sem, value) for sem, value in waits if not isinstance(value, int) or value > 0]
    waits = [(sem, value if isinstance(value, int) else eng.to_reg(value)) for sem, value in waits]
    eng.wait_ge(*met)
    for sem, value in waits:
        eng.wait_ge(sem, value)


def build(nc, tokens, emb, proj, ln_w, ln_b, wq, wk, wv, wo, router, gate_up, down, out):
    xs = nc.dram_tensor("normed_tokens", (TOKENS, XW), F32).ap()

    ctx = ExitStack()
    with ctx:
        def sb(name, shape, dt=F32):
            return ctx.enter_context(nc.sbuf_tensor(name, shape, dt))

        def sem(name):
            return ctx.enter_context(nc.semaphore(name))

        bank = [ctx.enter_context(nc.psum_tensor(f"bank{n}", [P, 512], F32)) for n in range(8)]

        ident = sb("ident", [P, P])
        identb = sb("identb", [P, P], BF16)
        identh = sb("identh", [P, P], F16)
        causal = sb("causal", [P, QH * P], BF16)
        headmask = sb("headmask", [P, 8])
        before = sb("before", [P, P], BF16)
        onesb = sb("onesb", [P, P], BF16)
        iota_lo = sb("iota_lo", [P, P])
        iota_tile = sb("iota_tile", [P, TILES])
        trash_row = sb("trash_row", [P, 1])
        iota_pair = sb("iota_pair", [P, PAIRS])
        place1 = sb("place1", [P, 1])
        iota_expert = sb("iota_expert", [P, EXPERTS])
        ln_mul = sb("ln_mul", [P, 2])
        ln_add = sb("ln_add", [P, 2])
        minus_half = sb("minus_half", [P, 2])

        proj_s = sb("proj_s", [P, D])
        wqk_s = sb("wqk_s", [P, KC, 2 * D])
        wv_s = sb("wv_s", [P, KC, D])
        wo_s = sb("wo_s", [P, KC, D])
        lnw_s = sb("lnw_s", [P, KC])
        lnb_s = sb("lnb_s", [P, KC])
        rw_s = sb("rw_s", [P, KC, RN])
        gu_all = sb("gu_all", [P, EXPERTS * KC * 2 * UNIT])
        gu_s = gu_all[:, :].rearrange("p (e c h n) -> p e c h n", e=EXPERTS, c=KC, h=2)
        gu_parts = gu_all[:, :].bitcast(F16).rearrange("p (e c h v n) -> p e c h v n", e=EXPERTS, c=KC, h=2, v=2)
        down_all = sb("down_all", [P, EXPERTS * 2 * DOWN_UNIT])
        down_s = down_all[:, :].rearrange("p (e h n) -> p e h n", e=EXPERTS, h=2)
        down_parts = down_all[:, :].bitcast(F16).rearrange("p (e h v n) -> p e h v n", e=EXPERTS, h=2, v=2)
        scaled = sb("scaled", [P, 2 * UNIT + DOWN_UNIT])
        count_lo = scaled[:, D:D + P].bitcast(I32)
        count_place = scaled[:, D + P:D + P + 1].bitcast(I32)
        count_expert = scaled[:, D + 2 * P:D + 2 * P + EXPERTS].bitcast(I32)
        unit_max = sb("unit_max", [P, 2, 4])
        part_max = sb("part_max", [P, 2])
        expert_max = sb("expert_max", [P, 2])
        exponent_i = sb("exponent_i", [P, 2], I32)
        exponent = sb("exponent", [P, 2])
        weight_scale = sb("weight_scale", [P, 2])
        exponents = sb("exponents", [P, EXPERTS, 2])
        tok_s = sb("tok_s", [P, SEQS], I32)
        hash_s = sb("hash_s", [P, SEQS, 2], I32)
        new_base = sb("new_base", [P, D])
        base = sb("base", [P, 2, D])
        hidden = sb("hidden", [P, 2, D])
        place_of = sb("place_of", [P, EXPERTS], U32)

        REGION = 8192
        region = sb("region", [P, REGION])
        used = [0]

        def part(*shape, dt=F32):
            n = 1
            for s in shape:
                n *= s
            words = n if dt not in (BF16, F16) else n // 2
            a = region[:, used[0]:used[0] + words]
            used[0] += words
            assert used[0] <= REGION
            if dt != F32:
                a = a.bitcast(dt)
            if len(shape) == 2:
                a = a.rearrange("p (a b) -> p a b", a=shape[0])
            if len(shape) == 3:
                a = a.rearrange("p (a b c) -> p a b c", a=shape[0], b=shape[1])
            return a

        pair_emb = part(2, 2 * RANK)
        emb_t = part(P)
        z = part(D)
        y_t = part(KC, P)
        q_masked = part(HEADS, P)
        k_t = part(2, KC, P)
        v_one = part(2, HEADS * VW + AVN)
        probs = part(2, QH * P)
        probs_t = part(2, QH * P)
        attn = part(D)
        attn_t = part(KC, P)
        x2 = sb("x2", [P, 2, D])
        x_row = sb("x_row", [P, 2 * XW])
        x_out = x_row[:, :].rearrange("p (u n) -> p u n", u=2)
        x_parts = x_row[:, :].bitcast(F16).rearrange("p (u n) -> p u n", u=2)
        logit = part(EXPERTS)
        sorted_l = part(EXPERTS)
        sorted_x = part(EXPERTS)
        exp_sum = part(1)
        exp_rec = part(1)
        x2_t = part(KC, P)
        minus_max = part(2, QH)
        recip = part(HEADS)
        bnF, mvF, aF, rF, nmF = part(6), part(2), part(2), part(2), part(2)
        bnO, mvO, aO, rO, nmO = part(6), part(2), part(2), part(2), part(2)
        gathered_idx = sb("gathered_idx", [P, 2, 2], I32)

        used[0] = 0
        NE = SEQS * EXPERTS
        tab = part(2, TILES)
        pair_i, half_i = part(TILES, dt=I32), part(TILES, dt=I32)
        half_f, place_f, empty = part(TILES), part(TILES), part(TILES)
        ends, ends2, starts = part(EXPERTS), part(EXPERTS), part(EXPERTS)
        cmp_f = part(TILES, EXPERTS)
        exp_f = part(TILES)
        steps_e = part(2, EXPERTS - 1)
        steps_t = part(TILES, EXPERTS - 1)
        exponent_t = part(2, TILES)
        gain, gain2 = part(TILES), part(TILES)
        late = used[0]
        count_i, tiles_i = part(EXPERTS, dt=I32), part(EXPERTS, dt=I32)
        slots = part(SEQS, EXPERTS)
        chosen_slots = part(PAIRS, EXPERTS)
        pos_f, pos_i = part(PAIRS), part(PAIRS, dt=I32)
        hi_i, lo_i = part(PAIRS, dt=I32), part(PAIRS, dt=I32)
        onehot_lo = part(2, GROUP * P, dt=BF16)
        onehot_hi = part(2, GROUP * 72)
        onehot_hv = part(2, 2 * GROUP * 72, dt=BF16)
        chosen_mask = sb("chosen_mask", [P, SEQS, 2, EXPERTS])
        both_h = sb("both_h", [P, SEQS, EXPERTS], BF16)
        cum_h = sb("cum_h", [P, SEQS + 1, EXPERTS], BF16)
        second = sb("second", [P, TILES])
        first = sb("first", [P, TILES])
        slot_w = sb("slot_w", [P, TILES])
        w_part = sb("w_part", [P, 1])
        tok_of = sb("tok_of", [P, TILES], I32)
        row_of = sb("row_of", [P, TILES], I32)
        exp_of = sb("exp_of", [1, TILES], I32)

        gate_gain = sb("gate_gain", [P, TILES])
        up_gain = sb("up_gain", [P, TILES])

        used[0] = late
        tok_idx = sb("tok_idx", [P, 2], I32)
        row_idx = sb("row_idx", [P, 2], I32)
        xe_all = part(2 * XW)
        xe = xe_all.rearrange("p (u n) -> p u n", u=2)
        xe_parts = xe_all.bitcast(F16).rearrange("p (u n) -> p u n", u=2)
        xe_t = part(2, 2 * KC * P, dt=F16)
        silu = part(2, HALF)
        h_s = part(2, HALF)
        h_hi, h_lo = part(2, 3 * P, dt=F16), part(2, 3 * P, dt=F16)
        y_s = part(2, D)
        turned_x = bank[7][:, :].bitcast(F16)

        ld_tok, ld_att, ld_exp = sem("ld_tok"), sem("ld_att"), sem("ld_exp")
        const_v, const_p, const_q = sem("const_v"), sem("const_p"), sem("const_q")
        hashed = sem("hashed")
        idx_ready = sem("idx_ready")
        emb_in = [sem("emb_in0"), sem("emb_in1")]
        embT_ps, embT_sb, h_ps = sem("embT_ps"), sem("embT_sb"), sem("h_ps")
        f_bn, f_mv, f_a, f_pow, f_nm, f_r1, z_sb, sum_sb, base_sb = (
            sem(n) for n in ("f_bn", "f_mv", "f_a", "f_pow", "f_nm", "f_r1", "z_sb", "sum_sb", "base_sb"))
        zT_ps, yT_sb, qk_ps, k_sb, q_sb, v_ps, v_sb = (
            sem(n) for n in ("zT_ps", "yT_sb", "qk_ps", "k_sb", "q_sb", "v_ps", "v_sb"))
        s_ps, max_sb, exp_sb, pT_ps, pT_sb, av_ps = (
            sem(n) for n in ("s_ps", "max_sb", "exp_sb", "pT_ps", "pT_sb", "av_ps"))
        rec_sb, attn_sb, attnT_ps, attnT_sb, o_ps, hid_sb = (
            sem(n) for n in ("rec_sb", "attn_sb", "attnT_ps", "attnT_sb", "o_ps", "hid_sb"))
        o_bn, o_mv, o_a, o_pow, o_nm, x2_sb = (
            sem(n) for n in ("o_bn", "o_mv", "o_a", "o_pow", "o_nm", "x2_sb"))
        x2_out = [sem("x2_out0"), sem("x2_out1")]
        x2T_ps, x2T_sb, lg_ps, lg_sb = sem("x2T_ps"), sem("x2T_sb"), sem("lg_ps"), sem("lg_sb")
        c_max, c_idx, c_sub, c_exp, c_rec, c_w = (
            sem(n) for n in ("c_max", "c_idx", "c_sub", "c_exp", "c_rec", "c_w"))
        part_sb, max_part, max_all, e_int, e_sb, scale_sb, e_put = (
            sem(n) for n in ("part_sb", "max_part", "max_all", "e_int", "e_sb", "scale_sb", "e_put"))
        scaled_sb, w_hi, w_lo = sem("scaled_sb"), sem("w_hi"), sem("w_lo")
        x_hi, x_lo = sem("x_hi"), sem("x_lo")
        h_clear, hi_sb = sem("h_clear"), sem("hi_sb")
        hid_out = [sem("hid_out0"), sem("hid_out1")]
        zero_sb, zero_out = sem("zero_sb"), sem("zero_out")
        route, rank_ps = sem("route"), sem("rank_ps")
        oh_lo, oh_hi, oh_hp, oh_hc, tab_mm = (
            sem(n) for n in ("oh_lo", "oh_hi", "oh_hp", "oh_hc", "tab_mm"))
        m_sb, both_sb, counted = sem("m_sb"), sem("both_sb"), sem("counted")
        tile_sb, tok_sb, row_sb, gain_sb = sem("exp_of_sb"), sem("tok_sb"), sem("row_sb"), sem("gain_sb")
        tidx, ridx = sem("tidx"), sem("ridx")
        xe_in = [sem("xe_in0"), sem("xe_in1")]
        xeT_ps, xeT_sb = sem("xeT_ps"), sem("xeT_sb")
        gu_ps, silu_sb, hid2_sb, hT_ps, hT_sb, y_ps, y_sb = (
            sem(n) for n in ("gu_ps", "silu_sb", "hid2_sb", "hT_ps", "hT_sb", "y_ps", "y_sb"))
        w_half, w_slot = sem("w_half"), sem("w_slot")
        y_out = sem("y_out")

        block = ctx.enter_context(nc.Block())

        S = [bank[0], bank[1]]
        PT = [bank[2], bank[3]]
        AV, FB, VB, OB = bank[4], bank[5], bank[6], bank[7]
        N_ATT = 16 * 9
        N_CONST = 14

        def sequence(i):
            return At(i // 2, i % 2) if 0 <= i < SEQS else None

        FIRST_I = 2 * FIRST_K
        LAST_I = FIRST_I + 2 * EXPERTS

        def unit_of(i, since):
            n = i - since
            return At(n // 2, n % 2) if 0 <= n < 2 * EXPERTS else None

        def run_sequences(step, eng):
            def straight(first, last):
                for i in range(first, last):
                    step(*(sequence(i + d) for d in (2, 1, 0, -1, -2)), unit_of(i, FIRST_I), unit_of(i, FIRST_I + 2))

            def loop(first, last, units):
                with eng.Fori(first // 2, last // 2) as k:
                    for u in range(2):
                        measured = At(k - FIRST_K, u) if units else None
                        split = At(k - FIRST_K - 1, u) if units else None
                        step(*(At(k, u).plus(d) for d in (2, 1, 0, -1, -2)), measured, split)

            straight(-2, 4)
            loop(4, FIRST_I, False)
            straight(FIRST_I, FIRST_I + 4)
            loop(FIRST_I + 4, LAST_I, True)
            straight(LAST_I, LAST_I + 2)
            loop(LAST_I + 2, SEQS - 2, False)
            straight(SEQS - 2, SEQS + 2)

        def weight_units(at):
            units = [(scaled[:, half * UNIT:(half + 1) * UNIT], gu_parts[:, at.k, at.u, half, 0, :],
                      gu_parts[:, at.k, at.u, half, 1, :]) for half in range(2)]
            return units + [(scaled[:, 2 * UNIT:], down_parts[:, at.k, at.u, 0, :], down_parts[:, at.k, at.u, 1, :])]

        def tile_at(t):
            return At(t // 2, t % 2) if 0 <= t < TILES else None

        def run_tiles(step, eng):
            for t in range(4):
                step(*(tile_at(t + d) for d in (-1, 0, 1, 2)))
            with eng.Fori(2, (TILES - 3) // 2) as k:
                for u in range(2):
                    step(*(At(k, u).plus(d) for d in (-1, 0, 1, 2)))
            for t in range(2 * ((TILES - 3) // 2), TILES + 1):
                step(*(tile_at(t + d) for d in (-1, 0, 1, 2)))

        @block.sync
        def _(eng):
            eng.dma_start(tok_s[:, :], tokens).then_inc(ld_tok, 16)
            eng.dma_start(proj_s[0:RANK, :], proj).then_inc(ld_att, 16)
            eng.dma_start(proj_s[RANK:P, :], proj).then_inc(ld_att, 16)
            eng.dma_start(lnw_s[:, :], ln_w).then_inc(ld_att, 16)
            eng.dma_start(lnb_s[:, :], ln_b).then_inc(ld_att, 16)
            eng.dma_start(wqk_s[:, :, 0:D], wq).then_inc(ld_att, 16)
            eng.dma_start(wqk_s[:, :, D:2 * D], wk).then_inc(ld_att, 16)
            eng.dma_start(wv_s[:, :, :], wv).then_inc(ld_att, 16)
            eng.dma_start(wo_s[:, :, :], wo).then_inc(ld_att, 16)
            eng.dma_start(rw_s[:, :, :], router).then_inc(ld_att, 16)

            eng.wait_ge(zero_sb, 1)
            eng.dma_start(out[TOKENS:TOKENS + P, :], scaled[:, 0:D]).then_inc(zero_out, 16)

            def store(at):
                eng.wait_ge(hid_sb, at.i + 1)
                eng.dma_start(out[bass.ds(at.i * SEQ, SEQ), :], hidden[:, at.u, :]).then_inc(hid_out[at.u], 16)
                eng.wait_ge(x_lo, at.i + 1)
                eng.wait_ge(c_w, at.i + 1)
                eng.dma_start(xs[bass.ds(at.i * SEQ, SEQ), :], x_out[:, at.u, :]).then_inc(x2_out[at.u], 16)

            def load_expert(e):
                eng.dma_start(gu_s[:, e], gate_up[:, e]).then_inc(ld_exp, 16)
                eng.dma_start(down_s[:, e], down[:, e]).then_inc(ld_exp, 16)

            eng.wait_ge(emb_in[1], 32)
            load_expert(0)
            load_expert(1)
            for i in range(EXPERTS - 2):
                store(sequence(i))
                load_expert(i + 2)
            with eng.Fori((EXPERTS - 2) // 2, SEQS // 2) as k:
                store(At(k, 0))
                store(At(k, 1))

            eng.wait_ge(y_out, 16 * TILES)

        @block.gpsimd
        def _(eng):
            eng.memset(ident[:, :], 0.0).then_inc(const_p, 1)
            eng.memset(headmask[:, :], SCALE).then_inc(const_p, 1)
            eng.memset(causal[:, :], 0.0).then_inc(const_p, 1)
            eng.memset(before[:, :], 1.0).then_inc(const_p, 1)
            eng.memset(minus_half[:, :], -0.5).then_inc(const_p, 1)
            eng.iota(row_of[:, :], pattern=[[1, TILES]], base=0, channel_multiplier=0).then_inc(const_p, 1)
            eng.iota(count_lo, pattern=[[1, P]], base=0, channel_multiplier=0).then_inc(const_p, 1)
            eng.iota(count_place, pattern=[[1, 1]], base=1, channel_multiplier=1).then_inc(const_p, 1)
            eng.iota(count_expert, pattern=[[1, EXPERTS]], base=0, channel_multiplier=0).then_inc(const_p, 1)
            eng.wait_ge(const_p, 9)
            eng.affine_select(out=ident[:, :], in_=ident[:, :], compare_op=ALU.not_equal, fill=1.0, base=0,
                              pattern=[[-1, P]], channel_multiplier=1).then_inc(const_q, 1)
            eng.affine_select(out=causal[:, :], in_=causal[:, :], compare_op=ALU.is_ge, fill=NEG, base=0,
                              pattern=[[0, QH], [-1, P]], channel_multiplier=1).then_inc(const_q, 1)
            eng.affine_select(out=before[:, :], in_=before[:, :], compare_op=ALU.is_gt, fill=0.0, base=0,
                              pattern=[[1, P]], channel_multiplier=-1).then_inc(const_q, 1)
            eng.affine_select(out=headmask[:, :], in_=headmask[:, :], compare_op=ALU.is_ge, fill=0.0, base=0,
                              pattern=[[-HD, 8]], channel_multiplier=1).then_inc(const_q, 1)
            eng.wait_ge(const_q, 4)
            eng.affine_select(out=headmask[:, :], in_=headmask[:, :], compare_op=ALU.is_ge, fill=0.0, base=HD - 1,
                              pattern=[[HD, 8]], channel_multiplier=-1).then_inc(const_q, 1)
            eng.wait_ge(hashed, 5)

            def gather(at):
                wait(eng, embT_ps, at.i - 1)
                eng.tensor_copy(gathered_idx[:, at.u, :], hash_s[:, at.i, :]).then_inc(idx_ready, 1)
                waits_apart(eng, (hashed, 5), (idx_ready, at.i + 1))
                for c in range(2):
                    eng.indirect_dma_start(
                        out=pair_emb[:, at.u, c * RANK:(c + 1) * RANK], out_offset=None, in_=emb,
                        in_offset=bass.IndirectOffsetOnAxis(ap=gathered_idx[:, at.u, c:c + 1], axis=0),
                    ).then_inc(emb_in[at.u], 16)

            def second_weights(at, j):
                whole, hi, lo = weight_units(at)[j]
                waits_apart(eng, (hashed, 5), (w_hi, 3 * at.i + j + 1))
                eng.tensor_tensor(lo, whole, hi, ALU.subtract).then_inc(w_lo, 1)

            def step(early, front, mid, back, chosen, measured, split):
                if early is not None:
                    gather(early)
                if back is not None:
                    eng.wait_ge(o_a, back.i + 1)
                    eng.tensor_tensor(rO[:, 0:1], aO[:, 0:1], minus_half[:, 0:1], ALU.pow).then_inc(o_pow, 1)
                if front is not None:
                    waits_apart(eng, (hashed, 5), (sum_sb, front.i + 1), (hid_sb, front.i - 1))
                    eng.tensor_copy(base[:, front.u, :], new_base[:, :]).then_inc(base_sb, 1)
                if split is not None:
                    second_weights(split, 0)
                if back is not None:
                    waits_apart(eng, (hashed, 5), (x2_sb, back.i + 1), (x2_out[back.u], 16 * back.k))
                    eng.tensor_copy(x_parts[:, back.u, 0:D], x2[:, back.u, :]).then_inc(x_hi, 1)
                    waits_apart(eng, (hashed, 5), (x_hi, back.i + 1))
                    eng.tensor_tensor(x_parts[:, back.u, D:2 * D], x2[:, back.u, :], x_parts[:, back.u, 0:D],
                                      ALU.subtract).then_inc(x_lo, 1)
                if chosen is not None:
                    waits_apart(eng, (hashed, 5), (m_sb, chosen.i + 1))
                    eng.tensor_tensor(both_h[:, chosen.i, :], chosen_mask[:, chosen.i, 0, :], chosen_mask[:, chosen.i, 1, :],
                                      ALU.add).then_inc(both_sb, 1)
                    waits_apart(eng, (hashed, 5), (both_sb, chosen.i + 1), (counted, chosen.i))
                    eng.tensor_tensor(cum_h[:, chosen.i + 1, :], cum_h[:, chosen.i, :], both_h[:, chosen.i, :],
                                      ALU.add).then_inc(counted, 1)
                if split is not None:
                    second_weights(split, 1)
                    second_weights(split, 2)
                if early is not None:
                    eng.wait_ge(f_a, early.i + 1)
                    eng.tensor_tensor(rF[:, :], aF[:, :], minus_half[:, :], ALU.pow).then_inc(f_pow, 1)
                if measured is not None and measured.u == 1:
                    waits_apart(eng, (hashed, 5), (max_part, measured.k + 1), (e_int, measured.k))
                    eng.partition_all_reduce(expert_max[:, :], part_max[:, :], P, bass.bass_isa.ReduceOp.max).then_inc(max_all, 1)

            run_sequences(step, eng)

            def weigh(g, u):
                waits_apart(eng, (hashed, 5), (oh_hi, g + 1), (tab_mm, g - 1))
                hi = onehot_hi[:, u, 0:GROUP * TILES].rearrange("p (c t) -> p c t", c=GROUP)
                hv = onehot_hv[:, u, 0:2 * GROUP * TILES].rearrange("p (c v t) -> p c v t", c=GROUP, v=2)
                eng.tensor_tensor(hv[:, :, 1, :], hi,
                                  iota_pair[:, bass.ds(g * GROUP, GROUP)].unsqueeze(2).to_broadcast([P, GROUP, TILES]),
                                  ALU.mult).then_inc(oh_hc, 1)

            weigh(0, 0)
            weigh(1, 1)
            with eng.Fori(1, PAIRS // GROUP // 2) as k:
                weigh(2 * k, 0)
                weigh(2 * k + 1, 1)

            eng.wait_ge(tok_sb, 1)
            for u in range(2):
                eng.wait_ge(x2_out[u], 16 * (SEQS // 2))

            def fetch(at):
                wait(eng, xeT_ps, at.i - 1)
                wait(eng, w_slot, at.i - 1)
                eng.tensor_copy(tok_idx[:, at.u:at.u + 1], tok_of[:, bass.ds(at.i, 1)]).then_inc(tidx, 1)
                waits_apart(eng, (tok_sb, 1), (tidx, at.i + 1))
                eng.indirect_dma_start(
                    out=xe[:, at.u, :], out_offset=None, in_=xs,
                    in_offset=bass.IndirectOffsetOnAxis(ap=tok_idx[:, at.u:at.u + 1], axis=0),
                ).then_inc(xe_in[at.u], 16)

            def scatter(at):
                wait(eng, y_out, 16 * at.i)
                eng.tensor_copy(row_idx[:, at.u:at.u + 1], row_of[:, bass.ds(at.i, 1)]).then_inc(ridx, 1)
                waits_apart(eng, (tok_sb, 1), (ridx, at.i + 1))
                eng.wait_ge(y_sb, at.i + 1)
                eng.indirect_dma_start(
                    out=out, out_offset=bass.IndirectOffsetOnAxis(ap=row_idx[:, at.u:at.u + 1], axis=0),
                    in_=y_s[:, at.u, :], in_offset=None, compute_op=ALU.add,
                ).then_inc(y_out, 16)

            fetch(At(0, 0))
            fetch(At(0, 1))
            eng.wait_ge(row_sb, 1)
            for u in range(2):
                eng.wait_ge(hid_out[u], 16 * (SEQS // 2))
            eng.wait_ge(zero_out, 16)

            def step(prev, at, nxt, after):
                if at is not None and after is not None:
                    fetch(after)
                if prev is not None:
                    scatter(prev)

            run_tiles(step, eng)

        @block.tensor
        def _(eng):
            eng.wait_ge(const_q, 5)
            eng.wait_ge(const_v, N_CONST)
            eng.wait_ge(ld_att, N_ATT)

            def scores(at, q):
                n = 4 * at.i + q
                if q == 0:
                    eng.wait_ge(k_sb, at.i + 1)
                eng.wait_ge(q_sb, n + 1)
                wait(eng, exp_sb, n - 1)
                s = S[q % 2]
                eng.matmul(s[:, :], identb[:, :], causal[:, :], start=True, stop=False)
                for h in range(QH):
                    mm = eng.matmul(s[:, h * P:(h + 1) * P], q_masked[:, q * QH + h, :], k_t[:, at.u, q // 2, :],
                                    start=False, stop=(h == QH - 1))
                mm.then_inc(s_ps, 1)

            def probs_turn(at, q):
                n = 4 * at.i + q
                eng.wait_ge(exp_sb, n + 1)
                wait(eng, pT_sb, n - 1)
                for h in range(QH):
                    mm = eng.transpose(PT[q % 2][:, h * P:(h + 1) * P], probs[:, q % 2, h * P:(h + 1) * P], ident[:, :])
                mm.then_inc(pT_ps, 1)

            def weigh_values(at, q):
                n = 4 * at.i + q
                eng.wait_ge(pT_sb, n + 1)
                if q == 0:
                    eng.wait_ge(v_sb, at.i + 1)
                    wait(eng, attn_sb, at.i)
                for h in range(QH):
                    c = (q * QH + h) * VW
                    mm = eng.matmul(AV[:, c:c + AVN], probs_t[:, q % 2, h * P:(h + 1) * P], v_one[:, at.u, c:c + AVN],
                                    start=True, stop=True)
                mm.then_inc(av_ps, 1)

            def turn(dst, src, done):
                for c in range(KC):
                    mm = eng.transpose(dst[:, c * P:(c + 1) * P], src[:, c * P:(c + 1) * P], ident[:, :])
                mm.then_inc(done, 1)

            def step(early, front, mid, back, chosen, measured, split):
                if mid is not None:
                    probs_turn(mid, 0)
                    scores(mid, 2)
                if back is not None:
                    eng.wait_ge(attn_sb, back.i + 1)
                    wait(eng, lg_sb, back.i)
                    turn(OB, attn, attnT_ps)
                if mid is not None:
                    probs_turn(mid, 1)
                    weigh_values(mid, 0)
                if front is not None:
                    eng.wait_ge(z_sb, front.i + 1)
                    eng.wait_ge(sum_sb, front.i + 1)
                    turn(FB, z, zT_ps)
                if back is not None:
                    eng.wait_ge(attnT_sb, back.i + 1)
                    for c in range(KC):
                        mm = eng.matmul(OB[:, D:2 * D], attn_t[:, c, :], wo_s[:, c, :], start=(c == 0), stop=(c == KC - 1))
                    mm.then_inc(o_ps, 1)
                if mid is not None:
                    scores(mid, 3)
                if front is not None:
                    eng.wait_ge(yT_sb, front.i + 1)
                    for m in range(4):
                        for c in range(KC):
                            mm = eng.matmul(FB[:, m * P:(m + 1) * P], wqk_s[:, c, m * P:(m + 1) * P], y_t[:, c, :],
                                            start=(c == 0), stop=(c == KC - 1))
                    mm.then_inc(qk_ps, 1)
                if mid is not None:
                    probs_turn(mid, 2)
                    weigh_values(mid, 1)
                if front is not None:
                    wait(eng, v_sb, front.i)
                    for c in range(KC):
                        mm = eng.matmul(VB[:, 0:D], y_t[:, c, :], wv_s[:, c, :], start=(c == 0), stop=(c == KC - 1))
                    mm.then_inc(v_ps, 1)
                if mid is not None:
                    weigh_values(mid, 2)
                if front is not None:
                    scores(front, 0)
                if back is not None:
                    eng.wait_ge(x2_sb, back.i + 1)
                    turn(OB, x2[:, back.u, :], x2T_ps)
                if mid is not None:
                    probs_turn(mid, 3)
                if early is not None:
                    eng.wait_ge(emb_in[early.u], 32 * (early.k + 1))
                    wait(eng, q_sb, 4 * early.i)
                    wait(eng, k_sb, early.i)
                    eng.transpose(FB[:, 0:P], pair_emb[:, early.u, :], ident[:, :]).then_inc(embT_ps, 1)
                if front is not None:
                    scores(front, 1)
                if early is not None:
                    eng.wait_ge(embT_sb, early.i + 1)
                    eng.matmul(FB[:, P:P + D], emb_t[:, :], proj_s[:, :], start=True, stop=True).then_inc(h_ps, 1)
                if mid is not None:
                    weigh_values(mid, 3)
                if back is not None:
                    eng.wait_ge(x2T_sb, back.i + 1)
                    for c in range(KC):
                        mm = eng.matmul(OB[:, D:D + RN], x2_t[:, c, :], rw_s[:, c, :], start=(c == 0), stop=(c == KC - 1))
                    mm.then_inc(lg_ps, 1)

            run_sequences(step, eng)

            eng.wait_ge(counted, SEQS)
            bh = both_h[:, :, :].rearrange("p a b -> p (a b)")
            eng.matmul(bank[0][:, 0:NE], before[:, :], bh, start=True, stop=False)
            eng.matmul(bank[0][:, 0:NE], onesb[:, :], cum_h[:, 0:SEQS, :].rearrange("p a b -> p (a b)"), start=False, stop=True).then_inc(rank_ps, 1)
            eng.matmul(bank[1][:, 0:EXPERTS], onesb[:, :], cum_h[:, SEQS, :], start=True, stop=True).then_inc(rank_ps, 1)

            def fill(k, u, first=False, last=False):
                g = 2 * k + u
                eng.wait_ge(oh_lo, g + 1)
                eng.wait_ge(oh_hp, g + 1)
                eng.wait_ge(oh_hc, g + 1)
                for c in range(GROUP):
                    mm = eng.matmul(bank[2][:, 0:2 * TILES], onehot_lo[:, u, c * P:(c + 1) * P],
                                    onehot_hv[:, u, c * 2 * TILES:(c + 1) * 2 * TILES],
                                    start=(first and c == 0), stop=(last and c == GROUP - 1))
                mm.then_inc(tab_mm, 1)

            groups = PAIRS // GROUP
            fill(0, 0, first=True)
            fill(0, 1)
            with eng.Fori(1, groups // 2 - 1) as k:
                fill(k, 0)
                fill(k, 1)
            fill(groups // 2 - 1, 0)
            fill(groups // 2 - 1, 1, last=True)

            eng.wait_ge(tile_sb, 1)
            eng.wait_ge(w_lo, 6 * EXPERTS)
            eng.wait_ge(h_clear, 2)

            def tokens_turn(at):
                eng.wait_ge(xe_in[at.u], 16 * (at.k + 1))
                wait(eng, xeT_sb, at.i)
                for c in range(2 * KC):
                    mm = eng.transpose(turned_x[:, c * P:(c + 1) * P], xe_parts[:, at.u, c * P:(c + 1) * P], identh[:, :])
                mm.then_inc(xeT_ps, 1)

            def widen(at, e, half):
                if half == 0:
                    eng.wait_ge(xeT_sb, at.i + 1)
                wait(eng, hid2_sb, 2 * at.i + half - 1)
                for g in range(2):
                    for c in range(KC):
                        for x_part, w_part in ((0, 0), (0, 1), (1, 0)):
                            mm = eng.matmul(bank[2 * half + g][:, 0:HALF],
                                            xe_t[:, at.u, (x_part * KC + c) * P:(x_part * KC + c + 1) * P],
                                            gu_parts[:, e, c, half, w_part, g * HALF:(g + 1) * HALF],
                                            start=(c == 0 and x_part + w_part == 0),
                                            stop=(c == KC - 1 and x_part == 1))
                mm.then_inc(gu_ps, 1)

            def inner_turn(at, half):
                n = 2 * at.i + half
                eng.wait_ge(hid2_sb, n + 1)
                wait(eng, hT_sb, n - 1)
                for c, w in enumerate(CHUNKS):
                    mm = eng.transpose(bank[4 + half][0:w, c * P:(c + 1) * P], h_s[:, half, c * P:c * P + w], ident[:, :])
                mm.then_inc(hT_ps, 1)

            def narrow(at, e):
                eng.wait_ge(hT_sb, 2 * at.i + 2)
                wait(eng, y_sb, at.i)
                for half in range(2):
                    for c, w in enumerate(CHUNKS):
                        for h_part, w_part in ((h_hi, 0), (h_hi, 1), (h_lo, 0)):
                            mm = eng.matmul(bank[6][:, 0:D], h_part[0:w, half, c * P:(c + 1) * P],
                                            down_parts[0:w, e, half, w_part, c * D:(c + 1) * D],
                                            start=(half == 0 and c == 0 and h_part is h_hi and w_part == 0),
                                            stop=(half == 1 and c == 2 and h_part is h_lo))
                mm.then_inc(y_ps, 1)

            def expert_of(at):
                return eng.value_load(exp_of[0:1, bass.ds(at.i, 1)], min_val=0, max_val=EXPERTS - 1)

            tokens_turn(tile_at(0))

            def step(prev, at, nxt, after):
                if at is not None:
                    e = expert_of(at)
                    widen(at, e, 0)
                    widen(at, e, 1)
                if nxt is not None:
                    tokens_turn(nxt)
                if prev is not None:
                    narrow(prev, expert_of(prev))
                if at is not None:
                    inner_turn(at, 0)
                    inner_turn(at, 1)

            run_tiles(step, eng)

        @block.scalar
        def _(eng):
            eng.wait_ge(ld_att, N_ATT)

            def exps(at, q):
                n = 4 * at.i + q
                eng.wait_ge(max_sb, n + 1)
                wait(eng, pT_ps, n - 1)
                for h in range(QH):
                    act = eng.activation(probs[:, q % 2, h * P:(h + 1) * P], S[q % 2][:, h * P:(h + 1) * P], ACT.Exp,
                                         bias=minus_max[:, q % 2, h:h + 1])
                act.then_inc(exp_sb, 1)

            def scale_unit(at, j):
                waits_apart(eng, (hashed, 5), (scale_sb, at.k + 1), (w_lo, 3 * at.i + j - 2))
                whole = weight_units(at)[j][0]
                kind = j // 2
                unit = (gu_s[:, at.k, at.u, 0, :], gu_s[:, at.k, at.u, 1, :], down_s[:, at.k, at.u, :])[j]
                eng.activation(whole, unit, ACT.Identity, scale=weight_scale[:, kind:kind + 1]).then_inc(scaled_sb, 1)

            def first_part(at, j):
                waits_apart(eng, (hashed, 5), (scaled_sb, 3 * at.i + j + 1))
                whole, hi, _ = weight_units(at)[j]
                eng.copy(hi, whole).then_inc(w_hi, 1)

            def probs_copy(at, q):
                n = 4 * at.i + q
                eng.wait_ge(pT_ps, n + 1)
                wait(eng, av_ps, n - 1)
                eng.copy(probs_t[:, q % 2, :], PT[q % 2][:, :]).then_inc(pT_sb, 1)

            def step(early, front, mid, back, chosen, measured, split):
                if mid is not None:
                    probs_copy(mid, 0)
                if back is not None:
                    eng.wait_ge(attnT_ps, back.i + 1)
                    wait(eng, o_ps, back.i)
                    eng.copy(attn_t.rearrange("p a b -> p (a b)"), OB[:, 0:D]).then_inc(attnT_sb, 1)
                if mid is not None:
                    probs_copy(mid, 1)
                if front is not None:
                    eng.wait_ge(zT_ps, front.i + 1)
                    wait(eng, v_ps, front.i)
                    for c in range(KC):
                        act = eng.activation(y_t[:, c, :], FB[:, c * P:(c + 1) * P], ACT.Identity,
                                             bias=lnb_s[:, c:c + 1], scale=lnw_s[:, c:c + 1])
                    act.then_inc(yT_sb, 1)
                if chosen is not None:
                    eng.wait_ge(c_sub, chosen.i + 1)
                    eng.activation(sorted_x, sorted_x, ACT.Exp, accum_out=exp_sum).then_inc(c_exp, 1)
                if mid is not None:
                    exps(mid, 2)
                if split is not None:
                    scale_unit(split, 0)
                    scale_unit(split, 1)
                    first_part(split, 0)
                if front is not None:
                    eng.wait_ge(qk_ps, front.i + 1)
                    wait(eng, s_ps, 4 * front.i - 4)
                    eng.copy(k_t[:, front.u].rearrange("p a b -> p (a b)"), FB[:, 2 * P:4 * P]).then_inc(k_sb, 1)
                if mid is not None:
                    probs_copy(mid, 2)
                    exps(mid, 3)
                if split is not None:
                    scale_unit(split, 2)
                if front is not None:
                    eng.wait_ge(v_ps, front.i + 1)
                    wait(eng, av_ps, 4 * front.i - 4)
                    eng.copy(v_one[:, front.u, 0:HEADS * VW].rearrange("p (h v) -> p h v", v=VW)[:, :, 0:HD],
                             VB[:, 0:D].rearrange("p (h v) -> p h v", v=HD)).then_inc(v_sb, 1)
                if split is not None:
                    first_part(split, 1)
                    first_part(split, 2)
                if back is not None:
                    eng.wait_ge(x2T_ps, back.i + 1)
                    wait(eng, lg_ps, back.i)
                    eng.copy(x2_t.rearrange("p a b -> p (a b)"), OB[:, 0:D]).then_inc(x2T_sb, 1)
                if mid is not None:
                    probs_copy(mid, 3)
                if early is not None:
                    eng.wait_ge(embT_ps, early.i + 1)
                    wait(eng, h_ps, early.i)
                    eng.mul(emb_t[:, :], FB[:, 0:P], 0.5).then_inc(embT_sb, 1)
                if front is not None:
                    exps(front, 0)
                    exps(front, 1)

            run_sequences(step, eng)

            def weigh(g, u):
                waits_apart(eng, (hashed, 5), (oh_hi, g + 1), (tab_mm, g - 1))
                hi = onehot_hi[:, u, 0:GROUP * TILES].rearrange("p (c t) -> p c t", c=GROUP)
                hv = onehot_hv[:, u, 0:2 * GROUP * TILES].rearrange("p (c v t) -> p c v t", c=GROUP, v=2)
                eng.activation(hv[:, :, 0, :], hi, ACT.Identity, scale=place1[:, 0:1]).then_inc(oh_hp, 1)

            weigh(0, 0)
            weigh(1, 1)
            with eng.Fori(1, PAIRS // GROUP // 2) as k:
                weigh(2 * k, 0)
                weigh(2 * k + 1, 1)

            def turned(at):
                eng.wait_ge(xeT_ps, at.i + 1)
                wait(eng, gu_ps, 2 * at.i - 2)
                eng.copy(xe_t[:, at.u, :], turned_x[:, 0:2 * KC * P]).then_inc(xeT_sb, 1)

            turned(tile_at(0))

            def step(prev, at, nxt, after):
                if at is None:
                    return
                for half in range(2):
                    n = 2 * at.i + half
                    waits_apart(eng, (gain_sb, 2), (gu_ps, n + 1), (hid2_sb, n - 1))
                    eng.activation(silu[:, half, :], bank[2 * half][:, 0:HALF], ACT.Silu,
                                   scale=gate_gain[:, bass.ds(at.i, 1)]).then_inc(silu_sb, 1)
                if nxt is not None:
                    turned(nxt)
                for half in range(2):
                    n = 2 * at.i + half
                    eng.wait_ge(hT_ps, n + 1)
                    wait(eng, y_ps, at.i)
                    eng.copy(h_hi[:, half, :], bank[4 + half][:, 0:3 * P]).then_inc(hi_sb, 1)

            run_tiles(step, eng)

        @block.vector
        def _(eng):
            eng.memset(scaled[:, 0:D], 0.0).then_inc(zero_sb, 1)
            eng.memset(onesb[:, :], 1.0).then_inc(const_v, 1)
            eng.wait_ge(ld_tok, 16)
            eng.tensor_scalar(tok_s[:, :], tok_s[:, :], BUCKETS - 1, None, ALU.bitwise_and).then_inc(hashed, 1)
            eng.wait_ge(hashed, 1)
            eng.tensor_scalar(hash_s[:, :, 0], tok_s[:, :], 31.0, 7.0, ALU.mult, ALU.add).then_inc(hashed, 1)
            eng.tensor_scalar(hash_s[:, :, 1], tok_s[:, :], 131.0, 13.0, ALU.mult, ALU.add).then_inc(hashed, 1)
            eng.wait_ge(hashed, 3)
            for c in range(2):
                eng.tensor_scalar(hash_s[:, :, c], hash_s[:, :, c], BUCKETS - 1, None, ALU.bitwise_and).then_inc(hashed, 1)

            eng.memset(cum_h[:, 0, :], 0.0).then_inc(const_v, 1)
            eng.memset(ln_mul[:, 0:1], 1.0).then_inc(const_v, 1)
            eng.memset(ln_mul[:, 1:2], 1.0 + EPS).then_inc(const_v, 1)
            eng.memset(ln_add[:, 0:1], EPS).then_inc(const_v, 1)
            eng.memset(ln_add[:, 1:2], EPS * EPS).then_inc(const_v, 1)
            eng.wait_ge(const_p, 9)
            eng.tensor_scalar(trash_row[:, :], count_place, float(TOKENS - 1), None,
                              ALU.add).then_inc(const_v, 1)
            eng.tensor_copy(iota_tile[:, :], row_of[:, :]).then_inc(const_v, 1)
            eng.tensor_copy(iota_lo[:, :], count_lo).then_inc(const_v, 1)
            eng.tensor_copy(place1[:, :], count_place).then_inc(const_v, 1)
            eng.tensor_copy(iota_expert[:, :], count_expert).then_inc(const_v, 1)
            eng.wait_ge(const_q, 1)
            eng.tensor_copy(identb[:, :], ident[:, :]).then_inc(const_v, 1)
            eng.tensor_copy(identh[:, :], ident[:, :]).then_inc(const_v, 1)
            eng.wait_ge(const_v, 13)
            eng.tensor_copy(iota_pair[:, :], iota_lo[:, 0:PAIRS])
            eng.memset(v_one.rearrange("p a b -> p (a b)"), 1.0).then_inc(const_v, 1)

            def row_max(at, q):
                n = 4 * at.i + q
                eng.wait_ge(s_ps, n + 1)
                wait(eng, exp_sb, n - 1)
                eng.tensor_reduce(minus_max[:, q % 2, :], S[q % 2][:, :].rearrange("p (h t) -> p h t", h=QH), AX,
                                  ALU.max, negate=True).then_inc(max_sb, 1)

            def measure(at):
                if at.u == 0 and isinstance(at.k, int) and at.k == 0:
                    eng.wait_ge(ld_exp, 32 * EXPERTS)
                eng.tensor_reduce(unit_max[:, 0, 2 * at.u:2 * at.u + 2], gu_s[:, at.k, at.u], AX, ALU.max,
                                  apply_absolute_value=True).then_inc(part_sb, 1)

            def measure_down(at):
                eng.tensor_reduce(unit_max[:, 1, 2 * at.u:2 * at.u + 2],
                                  down_s[:, at.k, at.u].rearrange("p (a b) -> p a b", a=2), AX, ALU.max,
                                  apply_absolute_value=True).then_inc(part_sb, 1)
                if at.u == 1:
                    eng.wait_ge(part_sb, 4 * at.k + 4)
                    wait(eng, max_all, at.k)
                    eng.tensor_reduce(part_max[:, :], unit_max[:, :, :], AX, ALU.max).then_inc(max_part, 1)

            def scale_of(at):
                eng.wait_ge(max_all, at.k + 1)
                eng.tensor_scalar(exponent_i[:, :], expert_max[:, :].bitcast(I32), 23, None,
                                  ALU.arith_shift_right).then_inc(e_int, 1)
                eng.wait_ge(e_int, at.k + 1)
                wait(eng, e_put, at.k)
                eng.tensor_scalar(exponent[:, :], exponent_i[:, :], float(LEAST), None, ALU.max).then_inc(e_sb, 1)
                eng.wait_ge(e_sb, at.k + 1)
                wait(eng, scaled_sb, 6 * at.k)
                eng.tensor_scalar(weight_scale[:, :].bitcast(I32), exponent[:, :], -ONE_EXPONENT,
                                  (2 * BIAS - 1 + TOP) * ONE_EXPONENT, ALU.mult, ALU.add).then_inc(scale_sb, 1)
                eng.tensor_copy(exponents[:, at.k, :], exponent[:, :]).then_inc(e_put, 1)

            def queries(front, q):
                if q == 0:
                    eng.wait_ge(k_sb, front.i + 1)
                wait(eng, s_ps, 4 * front.i + q - 3)
                g = q // 2
                eng.tensor_tensor(q_masked[:, q * QH:(q + 1) * QH, :],
                                  FB[:, g * P:(g + 1) * P].unsqueeze(1).to_broadcast([P, QH, P]),
                                  headmask[:, (q % 2) * QH:(q % 2 + 1) * QH].unsqueeze(2).to_broadcast([P, QH, P]),
                                  ALU.mult).then_inc(q_sb, 1)

            h = FB[:, P:P + D]

            def step(early, front, mid, back, chosen, measured, split):
                if chosen is not None:
                    waits_apart(eng, (hashed, 5), (lg_sb, chosen.i + 1))
                    eng.max(sorted_l, logit).then_inc(c_max, 1)
                if front is not None:
                    eng.wait_ge(f_pow, front.i + 1)
                    eng.tensor_scalar(nmF[:, :], rF[:, :], mvF[:, 0:1], -1.0, ALU.mult, ALU.mult).then_inc(f_nm, 1)
                    eng.tensor_scalar(aF[:, 0:1], rF[:, 0:1], 1.0, None, ALU.add).then_inc(f_r1, 1)
                if front is not None:
                    eng.wait_ge(f_nm, front.i + 1)
                    wait(eng, zT_ps, front.i)
                    eng.tensor_scalar(z[:, :], h, rF[:, 1:2], nmF[:, 1:2], ALU.mult, ALU.add).then_inc(z_sb, 1)
                    eng.wait_ge(f_r1, front.i + 1)
                    wait(eng, base_sb, front.i)
                    eng.tensor_scalar(new_base[:, :], h, aF[:, 0:1], nmF[:, 0:1], ALU.mult, ALU.add).then_inc(sum_sb, 1)
                if chosen is not None:
                    eng.wait_ge(c_max, chosen.i + 1)
                    eng.tensor_scalar(sorted_x, sorted_l, sorted_l[:, 0:1], None, ALU.subtract).then_inc(c_sub, 1)
                    eng.max_index(place_of[:, :], sorted_l, logit).then_inc(c_idx, 1)
                if mid is not None:
                    row_max(mid, 2)
                if split is not None and split.u == 0:
                    scale_of(split)
                if chosen is not None:
                    eng.wait_ge(c_idx, chosen.i + 1)
                    eng.tensor_tensor(chosen_mask[:, chosen.i, :, :], iota_expert[:, :].unsqueeze(1).to_broadcast([P, 2, EXPERTS]),
                                      place_of[:, 0:2].unsqueeze(2).to_broadcast([P, 2, EXPERTS]),
                                      ALU.is_equal).then_inc(m_sb, 1)
                if measured is not None:
                    measure(measured)
                if back is not None:
                    eng.wait_ge(base_sb, back.i + 1)
                    eng.wait_ge(o_ps, back.i + 1)
                    wait(eng, hid_out[back.u], 16 * back.k)
                    eng.tensor_tensor(hidden[:, back.u, :], OB[:, D:2 * D], base[:, back.u, :], ALU.add).then_inc(hid_sb, 1)
                    waits_apart(eng, (hashed, 5), (hid_sb, back.i + 1))
                    eng.bn_stats(bnO[:, :], hidden[:, back.u, :]).then_inc(o_bn, 1)
                    waits_apart(eng, (hashed, 5), (o_bn, back.i + 1))
                    eng.bn_aggr(mvO[:, :], bnO[:, :]).then_inc(o_mv, 1)
                    eng.wait_ge(o_mv, back.i + 1)
                    eng.tensor_scalar(aO[:, 0:1], mvO[:, 1:2], EPS, X_SCALE ** -2, ALU.add, ALU.mult).then_inc(o_a, 1)
                if chosen is not None:
                    eng.wait_ge(c_exp, chosen.i + 1)
                    eng.reciprocal(exp_rec, exp_sum).then_inc(c_rec, 1)
                    eng.wait_ge(c_rec, chosen.i + 1)
                    eng.wait_ge(x_lo, chosen.i + 1)
                    eng.tensor_scalar(x_out[:, chosen.u, D:D + 2], sorted_x[:, 0:2], exp_rec, None, ALU.mult).then_inc(c_w, 1)
                if mid is not None:
                    row_max(mid, 3)
                if back is not None:
                    eng.wait_ge(o_pow, back.i + 1)
                    eng.tensor_scalar(nmO[:, 0:1], rO[:, 0:1], mvO[:, 0:1], -1.0, ALU.mult, ALU.mult).then_inc(o_nm, 1)
                if front is not None:
                    queries(front, 0)
                if back is not None:
                    eng.wait_ge(o_nm, back.i + 1)
                    wait(eng, x2T_ps, back.i - 1)
                    wait(eng, x_lo, back.i - 1)
                    eng.tensor_scalar(x2[:, back.u, :], hidden[:, back.u, :], rO[:, 0:1], nmO[:, 0:1], ALU.mult,
                                      ALU.add).then_inc(x2_sb, 1)
                if front is not None:
                    for q in range(1, QUARTERS):
                        queries(front, q)
                if measured is not None:
                    measure_down(measured)
                if front is not None:
                    row_max(front, 0)
                    row_max(front, 1)
                if early is not None:
                    waits_apart(eng, (hashed, 5), (h_ps, early.i + 1))
                    eng.bn_stats(bnF[:, :], h).then_inc(f_bn, 1)
                if mid is not None:
                    eng.wait_ge(av_ps, 4 * mid.i + 4)
                    o = AV[:, 0:HEADS * VW].rearrange("p (h v) -> p h v", v=VW)
                    eng.reciprocal(recip[:, :], o[:, :, HD]).then_inc(rec_sb, 1)
                if early is not None:
                    waits_apart(eng, (hashed, 5), (f_bn, early.i + 1))
                    eng.bn_aggr(mvF[:, :], bnF[:, :]).then_inc(f_mv, 1)
                if mid is not None:
                    eng.wait_ge(rec_sb, mid.i + 1)
                    wait(eng, attnT_ps, mid.i)
                    eng.tensor_tensor(attn.rearrange("p (h v) -> p h v", v=HD), o[:, :, 0:HD],
                                      recip.unsqueeze(2).to_broadcast([P, HEADS, HD]), ALU.mult).then_inc(attn_sb, 1)
                if early is not None:
                    eng.wait_ge(f_mv, early.i + 1)
                    eng.scalar_tensor_tensor(out=aF[:, :], in0=ln_mul[:, :], scalar=mvF[:, 1:2], in1=ln_add[:, :],
                                             op0=ALU.mult, op1=ALU.add).then_inc(f_a, 1)
                if back is not None:
                    eng.wait_ge(lg_ps, back.i + 1)
                    eng.tensor_scalar(logit, OB[:, D:D + EXPERTS], 1 / X_SCALE, None, ALU.mult).then_inc(lg_sb, 1)

            run_sequences(step, eng)

            steps = [0]

            def done(instruction):
                steps[0] += 1
                instruction.then_inc(route, 1)
                eng.wait_ge(route, steps[0])

            eng.wait_ge(rank_ps, 2)
            done(eng.tensor_scalar(count_i, bank[1][:, 0:EXPERTS], float(P - 1), None, ALU.add))
            done(eng.tensor_scalar(tiles_i, count_i, 7, None, ALU.arith_shift_right))
            for shift, a, b in ((1, tiles_i, ends), (2, ends, ends2), (4, ends2, ends)):
                steps[0] += 2
                eng.tensor_copy(b[:, 0:shift], a[:, 0:shift]).then_inc(route, 1)
                eng.tensor_tensor(b[:, shift:], a[:, shift:], a[:, 0:EXPERTS - shift], ALU.add).then_inc(route, 1)
                eng.wait_ge(route, steps[0])
            done(eng.tensor_tensor(starts, ends, tiles_i, ALU.subtract))
            done(eng.tensor_scalar(starts, starts, float(P), None, ALU.mult))
            done(eng.tensor_tensor(slots, bank[0][:, 0:NE].rearrange("p (a b) -> p a b", b=EXPERTS),
                                   starts.unsqueeze(1).to_broadcast([P, SEQS, EXPERTS]), ALU.add))
            done(eng.tensor_tensor(chosen_slots.rearrange("p (a c) b -> p a c b", c=2),
                                   slots.unsqueeze(2).to_broadcast([P, SEQS, 2, EXPERTS]), chosen_mask[:, :, :, :], ALU.mult))
            done(eng.tensor_reduce(pos_f, chosen_slots, AX, ALU.add))
            done(eng.tensor_copy(pos_i, pos_f))
            done(eng.tensor_scalar(hi_i, pos_i, 7, None, ALU.arith_shift_right))
            done(eng.tensor_scalar(lo_i, pos_i, P - 1, None, ALU.bitwise_and))

            def onehots(g, u):
                wait(eng, tab_mm, g - 1)
                lo = lo_i[:, bass.ds(g * GROUP, GROUP)]
                hi = hi_i[:, bass.ds(g * GROUP, GROUP)]
                eng.tensor_tensor(onehot_hi[:, u, 0:GROUP * TILES].rearrange("p (c t) -> p c t", c=GROUP),
                                  iota_tile[:, :].unsqueeze(1).to_broadcast([P, GROUP, TILES]),
                                  hi.unsqueeze(2).to_broadcast([P, GROUP, TILES]), ALU.is_equal).then_inc(oh_hi, 1)
                eng.tensor_tensor(onehot_lo[:, u, :].rearrange("p (c t) -> p c t", c=GROUP),
                                  iota_lo[:, :].unsqueeze(1).to_broadcast([P, GROUP, P]),
                                  lo.unsqueeze(2).to_broadcast([P, GROUP, P]), ALU.is_equal).then_inc(oh_lo, 1)

            onehots(0, 0)
            onehots(1, 1)
            with eng.Fori(1, PAIRS // GROUP // 2) as k:
                onehots(2 * k, 0)
                onehots(2 * k + 1, 1)

            done(eng.tensor_tensor(cmp_f, iota_tile[:, :].unsqueeze(2).to_broadcast([P, TILES, EXPERTS]),
                                   ends.unsqueeze(1).to_broadcast([P, TILES, EXPERTS]), ALU.is_ge))
            done(eng.tensor_reduce(exp_f, cmp_f, AX, ALU.add))
            eng.tensor_scalar(exp_of[:, :], exp_f[0:1, :], float(EXPERTS - 1), None, ALU.min).then_inc(tile_sb, 1)
            eng.wait_ge(tab_mm, PAIRS // GROUP)
            done(eng.tensor_copy(tab.rearrange("p a b -> p (a b)"), bank[2][:, 0:2 * TILES]))
            place, pair = tab[:, 0, :], tab[:, 1, :]
            done(eng.tensor_copy(pair_i, pair))
            done(eng.tensor_scalar(half_i, pair_i, 1, None, ALU.arith_shift_right))
            done(eng.tensor_copy(half_f, half_i))
            done(eng.tensor_scalar(place_f, place, -1.0, 0.0, ALU.add, ALU.max))
            done(eng.scalar_tensor_tensor(out=place_f, in0=half_f, scalar=float(P), in1=place_f, op0=ALU.mult, op1=ALU.add))
            eng.tensor_copy(tok_of[:, :], place_f).then_inc(tok_sb, 1)
            done(eng.tensor_scalar(empty, place, 0.0, trash_row[:, 0:1], ALU.is_equal, ALU.mult))
            eng.tensor_tensor(row_of[:, :], empty, place_f, ALU.add).then_inc(row_sb, 1)
            eng.wait_ge(e_put, EXPERTS)
            by_kind = exponents[:, :, :].rearrange("p e v -> p v e")
            done(eng.tensor_tensor(steps_e, by_kind[:, :, 1:], by_kind[:, :, 0:EXPERTS - 1], ALU.subtract))
            for v in range(2):
                done(eng.tensor_tensor(steps_t, cmp_f[:, :, 0:EXPERTS - 1],
                                       steps_e[:, v, :].unsqueeze(1).to_broadcast([P, TILES, EXPERTS - 1]), ALU.mult))
                done(eng.tensor_reduce(exponent_t[:, v, :], steps_t, AX, ALU.add))
                done(eng.tensor_scalar(exponent_t[:, v, :], exponent_t[:, v, :], exponents[:, 0, v:v + 1], None, ALU.add))
            for target, kind, sign, add in ((gate_gain[:, :], 0, 1, 1 - X_EXP - TOP),
                                            (up_gain[:, :], 0, -1, 2 * BIAS - 2 - X_EXP - TOP),
                                            (gain, 0, 1, 1), (gain2, 1, 1, 2 - TOP)):
                done(eng.tensor_scalar(target.bitcast(I32), exponent_t[:, kind, :], sign * ONE_EXPONENT,
                                       add * ONE_EXPONENT, ALU.mult, ALU.add))
            for _ in range(2):
                done(eng.tensor_tensor(gain2, gain, gain2, ALU.mult))
            done(eng.scalar_tensor_tensor(out=second[:, :], in0=half_f, scalar=-2.0, in1=pair, op0=ALU.mult, op1=ALU.add))
            done(eng.tensor_scalar(first[:, :], second[:, :], -1.0, 1.0, ALU.mult, ALU.add))
            eng.tensor_tensor(first[:, :], first[:, :], gain2, ALU.mult).then_inc(gain_sb, 1)
            eng.tensor_tensor(second[:, :], second[:, :], gain2, ALU.mult).then_inc(gain_sb, 1)
            eng.wait_ge(gain_sb, 2)

            for half in range(2):
                eng.memset(bank[4 + half][CHUNKS[2]:P, 2 * P:3 * P], 0.0).then_inc(h_clear, 1)

            def product(at, half):
                n = 2 * at.i + half
                eng.wait_ge(silu_sb, n + 1)
                wait(eng, hT_ps, n - 1)
                eng.scalar_tensor_tensor(out=h_s[:, half, :], in0=bank[2 * half + 1][:, 0:HALF],
                                         scalar=up_gain[:, bass.ds(at.i, 1)], in1=silu[:, half, :], op0=ALU.mult,
                                         op1=ALU.mult).then_inc(hid2_sb, 1)

            def second_part(at, half):
                n = 2 * at.i + half
                eng.wait_ge(hi_sb, n + 1)
                wait(eng, y_ps, at.i)
                eng.tensor_tensor(h_lo[:, half, :], bank[4 + half][:, 0:3 * P], h_hi[:, half, :], ALU.subtract).then_inc(hT_sb, 1)

            def slot_weight(at):
                eng.wait_ge(xe_in[at.u], 16 * (at.k + 1))
                eng.tensor_tensor(w_part[:, :], xe[:, at.u, D:D + 1], first[:, bass.ds(at.i, 1)], ALU.mult).then_inc(w_half, 1)
                eng.wait_ge(w_half, at.i + 1)
                eng.scalar_tensor_tensor(out=slot_w[:, bass.ds(at.i, 1)], in0=xe[:, at.u, D + 1:D + 2],
                                         scalar=second[:, bass.ds(at.i, 1)], in1=w_part[:, :], op0=ALU.mult,
                                         op1=ALU.add).then_inc(w_slot, 1)

            def result(at):
                eng.wait_ge(y_ps, at.i + 1)
                wait(eng, y_out, 16 * (at.i - 1))
                eng.tensor_scalar(y_s[:, at.u, :], bank[6][:, 0:D], slot_w[:, bass.ds(at.i, 1)], None,
                                  ALU.mult).then_inc(y_sb, 1)

            def step(prev, at, nxt, after):
                if at is not None:
                    slot_weight(at)
                    product(at, 0)
                    product(at, 1)
                if prev is not None:
                    result(prev)
                if at is not None:
                    second_part(at, 0)
                    second_part(at, 1)

            run_tiles(step, eng)


def kernel(x, L0_tok_weight, L0_tok_proj, L0_attn_ln_w, L0_attn_ln_b, L0_attn_wq, L0_attn_wk, L0_attn_wv,
           L0_attn_wo, L0_ffn_router_w, L0_ffn_gate_w, L0_ffn_up_w, L0_ffn_down_w):
    import numpy as np
    import concourse.bacc as bacc
    from concourse.bass_utils import run_bass_kernel_spmd

    def chunks(a):
        return np.asarray(a).reshape(KC, P, -1).transpose(1, 0, 2)

    def heads(a):
        return np.asarray(a).transpose(1, 0, 2).reshape(D, D)

    router = np.zeros((D, RN), np.float32)
    router[:, :EXPERTS] = np.asarray(L0_ffn_router_w).T
    gate, up = (np.asarray(w).reshape(EXPERTS, 2, HALF, KC, P).transpose(4, 0, 3, 1, 2)
                for w in (L0_ffn_gate_w, L0_ffn_up_w))
    gate_up = np.stack([gate, up], axis=4)
    by_inner = np.asarray(L0_ffn_down_w).transpose(0, 2, 1)
    down = np.zeros((P, EXPERTS, 2 * len(CHUNKS), D), np.float32)
    for half in range(2):
        for c, w in enumerate(CHUNKS):
            at = half * HALF + c * P
            down[:w, :, 3 * half + c] = by_inner[:, at:at + w].transpose(1, 0, 2)
    arrays = {
        "tokens": np.asarray(x).T, "emb": L0_tok_weight, "proj": L0_tok_proj,
        "ln_w": np.asarray(L0_attn_ln_w).reshape(KC, P).T, "ln_b": np.asarray(L0_attn_ln_b).reshape(KC, P).T,
        "wq": chunks(heads(L0_attn_wq)), "wk": chunks(heads(L0_attn_wk)), "wv": chunks(heads(L0_attn_wv)),
        "wo": chunks(L0_attn_wo), "router": chunks(router), "gate_up": gate_up.reshape(P, EXPERTS, KC, 2, UNIT), "down": down.reshape(P, EXPERTS, 2, DOWN_UNIT),
    }
    nc = bacc.Bacc("TRN2", target_bir_lowering=False, num_devices=1)
    ins, args = {}, []
    for name, a in arrays.items():
        ins["in_" + name] = np.ascontiguousarray(a)
        args.append(nc.dram_tensor("in_" + name, ins["in_" + name].shape,
                                   mybir.dt.from_np(ins["in_" + name].dtype), kind="ExternalInput").ap())
    out = nc.dram_tensor("out_hidden", (TOKENS + P, D), F32, kind="ExternalOutput").ap()
    build(nc, *args, out)
    return run_bass_kernel_spmd(nc, [ins], core_ids=[0]).results[0]["out_hidden"][:TOKENS].reshape(SEQS, SEQ, D)
```
